# Optimizing a Trainium2 kernel written in Bass

```python
import numpy as np
import jax
import jax.numpy as jnp

def _softmax(x, axis=-1):
    return jax.nn.softmax(x, axis=axis)
def _gelu(x):
    return jax.nn.gelu(x, approximate=True)
def _silu(x):
    return jax.nn.silu(x)
def _sigmoid(x):
    return jax.nn.sigmoid(x)
def _layernorm(x, axis=-1, eps=1e-5):
    m = jnp.mean(x, axis=axis, keepdims=True)
    v = jnp.var(x, axis=axis, keepdims=True)
    return (x - m) / jnp.sqrt(v + eps)
def _scatter_add(tgt, idx, src, axis=0):
    return tgt.at[idx].add(src)
def _segment_sum(src, seg, n):
    return jax.ops.segment_sum(src, seg, n)

kernel_name = 'mk_conv_attn_hybrid_d2_conv_nchw256_ccca86'

def setup_inputs(seed: int = 0):
    np.random.seed(seed)
    _w = jnp.asarray
    def _rec_inputs():
        import jax
        import jax.numpy as jnp
        _gk = jax.random.key(seed)
        x = -0.0005153 + 1.001 * jax.random.normal(jax.random.fold_in(_gk, 1), (4, 256, 56, 56), jnp.float32)
        return x
    x = _rec_inputs()
    def _L0_conv_setup():
        import jax, jax.numpy as jnp
        import numpy as np
        K = 7
        D = 1
        PAD = 3
        N, CIN, H, Wd = (4, 256, 56, 56)
        REL, OUT, SHARE = (32, 256, 8)
        LOC = OUT // SHARE
        EPS = 1e-05

        def conv1x1(x, w, b=None):
            y = jnp.einsum('nc...,oc->no...', x, w)
            if b is not None:
                y = y + b.reshape((1, -1) + (1,) * (y.ndim - 2))
            return y

        def bn_eval(x, g, b, m, v):
            s = (1, -1) + (1,) * (x.ndim - 2)
            return (x - m.reshape(s)) * (g.reshape(s) * jax.lax.rsqrt(v.reshape(s) + EPS)) + b.reshape(s)

        def unfold_patches(x):
            h, w = (x.shape[2], x.shape[3])
            xp = jnp.pad(x, ((0, 0), (0, 0), (PAD, PAD), (PAD, PAD)), mode='reflect')
            return jnp.stack([xp[:, :, i * D:i * D + h, j * D:j * D + w] for i in range(K) for j in range(K)], axis=2)

        def position(h, w, dtype=jnp.float32):
            loc_w = jnp.tile(jnp.linspace(-1.0, 1.0, w, dtype=dtype)[None, :], (h, 1))
            loc_h = jnp.tile(jnp.linspace(-1.0, 1.0, h, dtype=dtype)[:, None], (1, w))
            return jnp.stack([loc_w, loc_h], axis=0)[None]
        key = jax.random.key(seed)
        ks = jax.random.split(key, 16)
        sc = 0.05
        inp = {'x': jax.random.normal(ks[0], (N, CIN, H, Wd), jnp.float32), 'w1': jax.random.normal(ks[1], (REL, CIN), jnp.float32) * sc, 'b1': jnp.zeros((REL,), jnp.float32), 'w2': jax.random.normal(ks[2], (REL, CIN), jnp.float32) * sc, 'b2': jnp.zeros((REL,), jnp.float32), 'w3': jax.random.normal(ks[3], (OUT, CIN), jnp.float32) * sc, 'b3': jnp.zeros((OUT,), jnp.float32), 'wp': jax.random.normal(ks[4], (2, 2), jnp.float32) * sc, 'bp': jnp.zeros((2,), jnp.float32), 'bn1_g': jnp.ones((REL + 2,), jnp.float32), 'bn1_b': jnp.zeros((REL + 2,), jnp.float32), 'bn1_m': jax.random.normal(ks[5], (REL + 2,), jnp.float32) * 0.01, 'bn1_v': jax.random.uniform(ks[6], (REL + 2,), jnp.float32, 0.5, 1.5), 'cw1': jax.random.normal(ks[7], (REL, REL + 2), jnp.float32) * sc, 'bn2_g': jnp.ones((REL,), jnp.float32), 'bn2_b': jnp.zeros((REL,), jnp.float32), 'bn2_m': jax.random.normal(ks[8], (REL,), jnp.float32) * 0.01, 'bn2_v': jax.random.uniform(ks[9], (REL,), jnp.float32, 0.5, 1.5), 'cw2': jax.random.normal(ks[10], (LOC, REL), jnp.float32) * sc, 'cb2': jnp.zeros((LOC,), jnp.float32)}
        return inp
    _L0_conv_all = _L0_conv_setup()
    _L0_conv_in = {k: v for k, v in _L0_conv_all.items() if k in ('w1', 'b1', 'w2', 'b2', 'w3', 'b3', 'wp', 'bp', 'bn1_g', 'bn1_b', 'bn1_m', 'bn1_v', 'cw1', 'bn2_g', 'bn2_b', 'bn2_m', 'bn2_v', 'cw2', 'cb2', )}
    del _L0_conv_all

    def _L1_attn_setup():
        import jax, jax.numpy as jnp
        import numpy as np
        NUM_HEADS = 8
        C_SHIFT = 5.0
        key = jax.random.key(seed)
        k1, k2, k3 = jax.random.split(key, 3)
        B, N, D = (8, 1024, 256)
        x = jax.random.normal(k1, (B, N, D), dtype=jnp.float32)
        qkv_w = jax.random.normal(k2, (3 * D, D), dtype=jnp.float32) * D ** (-0.5)
        qkv_b = jnp.zeros((3 * D,), dtype=jnp.float32)
        proj_w = jax.random.normal(k3, (D, D), dtype=jnp.float32) * D ** (-0.5)
        proj_b = jnp.zeros((D,), dtype=jnp.float32)
        return {'x': x, 'qkv_w': qkv_w, 'qkv_b': qkv_b, 'proj_w': proj_w, 'proj_b': proj_b}
    _L1_attn_all = _L1_attn_setup()
    _L1_attn_in = {k: v for k, v in _L1_attn_all.items() if k in ('qkv_w', 'qkv_b', 'proj_w', 'proj_b', )}
    del _L1_attn_all

    def _L1_ffn_setup():
        import jax, jax.numpy as jnp
        import numpy as np
        B, S, D = (8, 4096, 256)
        H = 4 * D
        CAPACITY = 0.5
        key = jax.random.key(seed)
        ks = jax.random.split(key, 6)
        x = jax.random.normal(ks[0], (B, S, D), dtype=jnp.float32)
        attention_mask = jnp.zeros((B, 1, 1, S), dtype=jnp.float32)
        wr = jax.random.normal(ks[1], (D, 1), dtype=jnp.float32) * 0.02
        br = jnp.zeros((1,), dtype=jnp.float32)
        w1 = jax.random.normal(ks[2], (D, H), dtype=jnp.float32) * 0.02
        b1 = jnp.zeros((H,), dtype=jnp.float32)
        w2 = jax.random.normal(ks[3], (H, D), dtype=jnp.float32) * 0.02
        b2 = jnp.zeros((D,), dtype=jnp.float32)
        return {'x': x, 'attention_mask': attention_mask, 'wr': wr, 'br': br, 'w1': w1, 'b1': b1, 'w2': w2, 'b2': b2}
    _L1_ffn_all = _L1_ffn_setup()
    _L1_ffn_in = {k: v for k, v in _L1_ffn_all.items() if k in ('attention_mask', 'wr', 'br', 'w1', 'b1', 'w2', 'b2', )}
    del _L1_ffn_all

    return {
        "x": x,
        "L0_conv_w1": _L0_conv_in["w1"],
        "L0_conv_b1": _L0_conv_in["b1"],
        "L0_conv_w2": _L0_conv_in["w2"],
        "L0_conv_b2": _L0_conv_in["b2"],
        "L0_conv_w3": _L0_conv_in["w3"],
        "L0_conv_b3": _L0_conv_in["b3"],
        "L0_conv_wp": _L0_conv_in["wp"],
        "L0_conv_bp": _L0_conv_in["bp"],
        "L0_conv_bn1_g": _L0_conv_in["bn1_g"],
        "L0_conv_bn1_b": _L0_conv_in["bn1_b"],
        "L0_conv_bn1_m": _L0_conv_in["bn1_m"],
        "L0_conv_bn1_v": _L0_conv_in["bn1_v"],
        "L0_conv_cw1": _L0_conv_in["cw1"],
        "L0_conv_bn2_g": _L0_conv_in["bn2_g"],
        "L0_conv_bn2_b": _L0_conv_in["bn2_b"],
        "L0_conv_bn2_m": _L0_conv_in["bn2_m"],
        "L0_conv_bn2_v": _L0_conv_in["bn2_v"],
        "L0_conv_cw2": _L0_conv_in["cw2"],
        "L0_conv_cb2": _L0_conv_in["cb2"],
        "L1_attn_qkv_w": _L1_attn_in["qkv_w"],
        "L1_attn_qkv_b": _L1_attn_in["qkv_b"],
        "L1_attn_proj_w": _L1_attn_in["proj_w"],
        "L1_attn_proj_b": _L1_attn_in["proj_b"],
        "L1_ffn_attention_mask": _L1_ffn_in["attention_mask"],
        "L1_ffn_wr": _L1_ffn_in["wr"],
        "L1_ffn_br": _L1_ffn_in["br"],
        "L1_ffn_w1": _L1_ffn_in["w1"],
        "L1_ffn_b1": _L1_ffn_in["b1"],
        "L1_ffn_w2": _L1_ffn_in["w2"],
        "L1_ffn_b2": _L1_ffn_in["b2"],
    }

def reference(x, L0_conv_w1, L0_conv_b1, L0_conv_w2, L0_conv_b2, L0_conv_w3, L0_conv_b3, L0_conv_wp, L0_conv_bp, L0_conv_bn1_g, L0_conv_bn1_b, L0_conv_bn1_m, L0_conv_bn1_v, L0_conv_cw1, L0_conv_bn2_g, L0_conv_bn2_b, L0_conv_bn2_m, L0_conv_bn2_v, L0_conv_cw2, L0_conv_cb2, L1_attn_qkv_w, L1_attn_qkv_b, L1_attn_proj_w, L1_attn_proj_b, L1_ffn_attention_mask, L1_ffn_wr, L1_ffn_br, L1_ffn_w1, L1_ffn_b1, L1_ffn_w2, L1_ffn_b2):
    import jax
    import jax.numpy as jnp
    def _L0_conv_ref(x, w1, b1, w2, b2, w3, b3, wp, bp, bn1_g, bn1_b, bn1_m, bn1_v, cw1, bn2_g, bn2_b, bn2_m, bn2_v, cw2, cb2):
        import jax, jax.numpy as jnp
        import numpy as np
        K = 7
        D = 1
        PAD = 3
        N, CIN, H, Wd = (4, 256, 56, 56)
        REL, OUT, SHARE = (32, 256, 8)
        LOC = OUT // SHARE
        EPS = 1e-05

        def conv1x1(x, w, b=None):
            y = jnp.einsum('nc...,oc->no...', x, w)
            if b is not None:
                y = y + b.reshape((1, -1) + (1,) * (y.ndim - 2))
            return y

        def bn_eval(x, g, b, m, v):
            s = (1, -1) + (1,) * (x.ndim - 2)
            return (x - m.reshape(s)) * (g.reshape(s) * jax.lax.rsqrt(v.reshape(s) + EPS)) + b.reshape(s)

        def unfold_patches(x):
            h, w = (x.shape[2], x.shape[3])
            xp = jnp.pad(x, ((0, 0), (0, 0), (PAD, PAD), (PAD, PAD)), mode='reflect')
            return jnp.stack([xp[:, :, i * D:i * D + h, j * D:j * D + w] for i in range(K) for j in range(K)], axis=2)

        def position(h, w, dtype=jnp.float32):
            loc_w = jnp.tile(jnp.linspace(-1.0, 1.0, w, dtype=dtype)[None, :], (h, 1))
            loc_h = jnp.tile(jnp.linspace(-1.0, 1.0, h, dtype=dtype)[:, None], (1, w))
            return jnp.stack([loc_w, loc_h], axis=0)[None]
        n, _, h, w = x.shape
        x1 = conv1x1(x, w1, b1)
        x2 = conv1x1(x, w2, b2)
        x3 = conv1x1(x, w3, b3)
        p = conv1x1(position(h, w, x.dtype), wp, bp)
        sub2 = x1[:, :, None] - unfold_patches(x2)
        subp = p[:, :, None] - unfold_patches(p)
        subp = jnp.broadcast_to(subp, (n,) + subp.shape[1:])
        feat = jnp.concatenate([sub2, subp], axis=1).reshape(n, REL + 2, K * K, h * w)
        y = jax.nn.relu(bn_eval(feat, bn1_g, bn1_b, bn1_m, bn1_v))
        y = conv1x1(y, cw1)
        y = jax.nn.relu(bn_eval(y, bn2_g, bn2_b, bn2_m, bn2_v))
        wgt = conv1x1(y, cw2, cb2)
        wgt = jax.nn.softmax(wgt, axis=2)
        wgt = wgt.reshape(n, LOC, K * K, h, w)
        x3p = jnp.pad(x3, ((0, 0), (0, 0), (PAD, PAD), (PAD, PAD)), mode='reflect')
        out = jnp.zeros((n, LOC, SHARE, h, w), x.dtype)
        idx = 0
        for i in range(K):
            for j in range(K):
                patch = x3p[:, :, i * D:i * D + h, j * D:j * D + w].reshape(n, LOC, SHARE, h, w)
                out = out + patch * wgt[:, :, idx][:, :, None]
                idx += 1
        return out.reshape(n, OUT, h, w)

    def _L1_attn_ref(x, qkv_w, qkv_b, proj_w, proj_b):
        import jax, jax.numpy as jnp
        import numpy as np
        NUM_HEADS = 8
        C_SHIFT = 5.0
        B, N, D = x.shape
        H = NUM_HEADS
        dh = D // H
        scale = dh ** (-0.5)
        qkv = x @ qkv_w.T + qkv_b
        qkv = qkv.reshape(B, N, 3, H, dh)
        q, k, v = (qkv[:, :, 0], qkv[:, :, 1], qkv[:, :, 2])
        scores = jnp.einsum('bnhd,bmhd->bhnm', q, k) * scale
        t = jnp.square(scores + C_SHIFT)
        attn = t / jnp.sum(t, axis=-1, keepdims=True)
        out = jnp.einsum('bhnm,bmhd->bnhd', attn, v).reshape(B, N, D)
        return out @ proj_w.T + proj_b

    def _L1_ffn_ref(x, attention_mask, wr, br, w1, b1, w2, b2):
        import jax, jax.numpy as jnp
        import numpy as np
        B, S, D = (8, 4096, 256)
        H = 4 * D
        CAPACITY = 0.5
        b, s, d = x.shape
        weights = (jnp.einsum('bsd,do->bso', x, wr) + br)[..., 0]
        k = max(1, int(CAPACITY * s))
        kk = k - 1 if k > 1 else 1
        _, idx = jax.lax.top_k(weights, k)
        sel_idx = idx[:, :kk]
        sel = jnp.take_along_axis(x, sel_idx[:, :, None], axis=1)
        h = jax.nn.gelu(jnp.einsum('bkd,dh->bkh', sel, w1) + b1)
        y = jnp.einsum('bkh,hd->bkd', h, w2) + b2
        w_sel = jnp.take_along_axis(weights, sel_idx, axis=1)
        y = y * w_sel[..., None]
        batch_idx = jnp.arange(b)[:, None]
        processed = jnp.zeros_like(x).at[batch_idx, sel_idx].set(y)
        return processed + x

    def _gn(v, G=32, eps=1e-5):
        B_, C_, H_, W_ = v.shape
        g = v.reshape(B_, G, C_ // G, H_, W_)
        m = jnp.mean(g, axis=(2, 3, 4), keepdims=True)
        s = jnp.var(g, axis=(2, 3, 4), keepdims=True)
        return ((g - m) / jnp.sqrt(s + eps)).reshape(v.shape)

    def _ln_c(v, eps=1e-6):
        m = jnp.mean(v, axis=1, keepdims=True)
        s = jnp.var(v, axis=1, keepdims=True)
        return (v - m) / jnp.sqrt(s + eps)

    def _ln_t(v, eps=1e-5):
        m = jnp.mean(v, axis=-1, keepdims=True)
        s = jnp.var(v, axis=-1, keepdims=True)
        return (v - m) / jnp.sqrt(s + eps)

    def _to_tokens(v):
        B_, C_, H_, W_ = v.shape
        return v.reshape(B_, C_, H_ * W_).transpose(0, 2, 1)
    def _from_tokens(t, like):
        B_, C_, H_, W_ = like.shape
        return t.transpose(0, 2, 1).reshape(B_, C_, H_, W_)

    x = x + _L0_conv_ref(_gn(x), L0_conv_w1, L0_conv_b1, L0_conv_w2, L0_conv_b2, L0_conv_w3, L0_conv_b3, L0_conv_wp, L0_conv_bp, L0_conv_bn1_g, L0_conv_bn1_b, L0_conv_bn1_m, L0_conv_bn1_v, L0_conv_cw1, L0_conv_bn2_g, L0_conv_bn2_b, L0_conv_bn2_m, L0_conv_bn2_v, L0_conv_cw2, L0_conv_cb2)
    t = _to_tokens(x)
    t = t + _L1_attn_ref(_ln_t(t), L1_attn_qkv_w, L1_attn_qkv_b, L1_attn_proj_w, L1_attn_proj_b)
    t = t + _L1_ffn_ref(_ln_t(t), L1_ffn_attention_mask, L1_ffn_wr, L1_ffn_br, L1_ffn_w1, L1_ffn_b1, L1_ffn_w2, L1_ffn_b2)
    x = _from_tokens(t, x)
    return x


_drawn_inputs = setup_inputs


def setup_inputs(seed=0):
    import zlib

    import numpy as np

    out = dict(_drawn_inputs(seed))
    spreads = {'L0_conv_b1': (0.0, 0.8),
     'L0_conv_b2': (0.0, 0.8),
     'L0_conv_b3': (0.0, 0.1),
     'L0_conv_bp': (0.0, 2.0),
     'L0_conv_bn1_g': (1.0, 0.6),
     'L0_conv_bn1_b': (0.0, 0.8),
     'L0_conv_bn2_g': (1.0, 0.6),
     'L0_conv_bn2_b': (0.0, 0.8),
     'L0_conv_cb2': (0.0, 2.0),
     'L1_attn_qkv_b': (0.0, 0.1),
     'L1_attn_proj_b': (0.0, 0.1),
     'L1_ffn_b1': (0.0, 0.8),
     'L1_ffn_b2': (0.0, 0.663)}
    factors = {'L0_conv_w1': 8.0,
     'L0_conv_w2': 8.0,
     'L0_conv_wp': 64.0,
     'L0_conv_bn1_m': 43.148,
     'L0_conv_bn1_v': 8.0,
     'L0_conv_cw1': 8.0,
     'L0_conv_bn2_m': 54.728,
     'L0_conv_bn2_v': 8.0,
     'L0_conv_cw2': 8.0,
     'L1_ffn_wr': 3.643,
     'L1_ffn_w1': 4.619,
     'L1_ffn_w2': 4.306}
    for name, (base, spread) in spreads.items():
        noise = np.random.default_rng([zlib.crc32(name.encode()), seed]).standard_normal(out[name].shape)
        drawn = base * np.exp(spread * noise) if base else spread * noise
        out[name] = jnp.asarray(drawn.astype(out[name].dtype))
    for name, factor in factors.items():
        out[name] = (out[name] * factor).astype(out[name].dtype)
    return out
```

```python
import numpy as np
import concourse.bass as bass
from concourse import mybir
from contextlib import ExitStack

F32 = mybir.dt.float32
BF16 = mybir.dt.bfloat16
ALU = mybir.AluOpType
ACT = mybir.ActivationFunctionType
AX = mybir.AxisListType

B, C, H, W = 4, 256, 56, 56
S = H * W
P = 128
CH = C // P
K7, PAD = 7, 3
REL = 32
SHARE = C // REL
WP = W + 2 * PAD
HP = H + 2 * PAD
NOUT = SHARE + 2
PL = SHARE + 1
RB = 8
NBK = H // RB
CB = RB * W
RW = 4
NW = H // RW
PW = RW * W
TAPS = K7 * K7
GC = 8
GN_EPS, BN_EPS = 1e-5, 1e-5

B1, B2, G1, BE1, M1, V1, G2, BE2, M2, V2, CB2, B3 = range(12)
NPAR = B3 + SHARE
WPX, WPY, BP, GP, BEP, MP, VP = range(7)


def project_stage(nc, x, par32, parp, proj_w, posw, posh, cw1pT, group_avg, planes, x2_dram, a1_dram, pf_dram, keep):
    ctx = ExitStack()
    with ctx:
        def sb(name, shape, dt=F32):
            return ctx.enter_context(nc.sbuf_tensor(name, shape, dt))

        def sem(name):
            return ctx.enter_context(nc.semaphore(name))

        xs = sb("xs", [P, B, CH, S])
        wts = sb("wts", [P, CH, NOUT, REL])
        gav = sb("gav", [P, P])
        stats = sb("stats", [P, B * CH, NBK, 6])
        mv = sb("mv", [P, B * CH, 2])
        mom = sb("mom", [P, 2, B * CH])
        gmom = sb("gmom", [P, 2, B * CH])
        gvar = sb("gvar", [P, B * CH])
        gstd = sb("gstd", [P, B * CH])
        grs = sb("grs", [P, B * CH])
        gnb = sb("gnb", [P, B * CH])
        stage = sb("stage", [P, 2, RB, PL, WP])
        a1s = sb("a1s", [P, 2, CB])
        fold = sb("fold", [P, 8])
        pwt = sb("pwt", [2 * H, 2, K7 * W])
        pht = sb("pht", [2 * H, 1 + K7])
        ppt = sb("ppt", [2 * H, 7])
        pq = sb("pq", [2 * H, 2, K7 * W])
        ud = sb("ud", [2 * H, K7 * W])
        hq = sb("hq", [2 * H, 1 + K7])
        vd = sb("vd", [2 * H, K7])
        pfold = sb("pfold", [2 * H, 3])
        feat = sb("feat", [2 * H, K7, K7 * W])
        fparts = sb("fparts", [2 * H, 3, K7, K7 * W], BF16)
        cwp = sb("cwp", [2, P])
        cwparts = sb("cwparts", [2, 3, P], BF16)
        ps = keep["ps"]

        par, cw1p18, s1c, t1c, t2c, s2c, u2c = (keep[k] for k in ("par", "cw1p18", "s1c", "t1c", "t2c", "s2c", "u2c"))

        x_in = [sem(f"x_in{n}") for n in range(B * CH)]
        small_in = sem("small_in")
        stat_done = sem("stat_done")
        mom_done = sem("mom_done")
        gmom_mm = sem("gmom_mm")
        gstep = sem("gstep")
        gsqrt = sem("gsqrt")
        fstep = sem("fstep")
        fsqrt = sem("fsqrt")
        normed = sem("normed")
        pstep = sem("pstep")
        feat_done = sem("feat_done")
        parts = sem("parts")
        proj_done = sem("proj_done")
        evac_a = sem("evac_a")
        evac_v = sem("evac_v")
        padded = sem("padded")
        stored = [sem(f"stored{k}") for k in range(2)]
        pf_out = sem("pf_out")
        cwp_out = sem("cwp_out")

        x_v = x.rearrange("b (k p) s -> b k p s", p=P)
        NPARTS = 6
        N_SMALL = 16 * (1 + 1 + 4 + 4 + 1 + 2 + 2)
        DVE_OUT = (3, 5, 7, 9)
        ACT_OUT = tuple(o for o in range(NOUT) if o not in DVE_OUT)
        block = ctx.enter_context(nc.Block())

        @block.sync
        def _(sp):
            for b in range(B):
                for k in range(CH):
                    sp.dma_start(xs[:, b, k, :], x_v[b, k]).then_inc(x_in[b * CH + k], 16)
            sp.wait_ge(parts, NPARTS)
            for f in range(3):
                for c in range(2):
                    sp.dma_start(pf_dram[2 * f + c].rearrange("i h x -> h i x"),
                                 fparts[c * H:(c + 1) * H, f]).then_inc(pf_out, 16)
            for w in range(3):
                for f in range(3):
                    sp.dma_start(cw1p18[w * 6 + f * 2:w * 6 + f * 2 + 2, :], cwparts[:, w, :]).then_inc(cwp_out, 16)
            for blk in range(NBK):
                s = blk % 2
                sp.wait_ge(evac_a, len(ACT_OUT) * (blk + 1))
                sp.wait_ge(evac_v, len(DVE_OUT) * (blk + 1))
                sp.wait_ge(padded, 2 * (blk + 1))
                r0 = PAD + blk * RB
                sp.dma_start(planes[:, r0:r0 + RB], stage[:, s, :, 0:SHARE]).then_inc(stored[s], 16)
                sp.dma_start(x2_dram[:, r0:r0 + RB], stage[:, s, :, SHARE]).then_inc(stored[s], 16)
                sp.dma_start(a1_dram[:, blk * CB:(blk + 1) * CB], a1s[:, s]).then_inc(stored[s], 16)
                if blk == 0:
                    for r in range(PAD):
                        sp.dma_start(planes[:, r], stage[:, s, PAD - r, 0:SHARE]).then_inc(stored[s], 16)
                        sp.dma_start(x2_dram[:, r], stage[:, s, PAD - r, SHARE]).then_inc(stored[s], 16)
                if blk == NBK - 1:
                    for r in range(PAD):
                        sp.dma_start(planes[:, PAD + H + r], stage[:, s, RB - 2 - r, 0:SHARE]).then_inc(stored[s], 16)
                        sp.dma_start(x2_dram[:, PAD + H + r], stage[:, s, RB - 2 - r, SHARE]).then_inc(stored[s], 16)
            sp.wait_ge(stored[0], 16 * (3 * ((NBK + 1) // 2) + 4 * PAD))
            sp.wait_ge(stored[1], 16 * (3 * (NBK // 2)))
            sp.wait_ge(pf_out, 16 * 6)
            sp.wait_ge(cwp_out, 16 * 9)

        @block.gpsimd
        def _(pool):
            pool.dma_start(wts[:], proj_w).then_inc(small_in, 16)
            pool.dma_start(gav[:], group_avg).then_inc(small_in, 16)
            for q in range(4):
                pool.dma_start(par[32 * q:32 * q + 32, :], par32).then_inc(small_in, 16)
                pool.dma_start(cwp[:, 32 * q:32 * q + 32], cw1pT).then_inc(small_in, 16)
            pool.dma_start(pwt[:], posw).then_inc(small_in, 16)
            for c in range(2):
                pool.dma_start(pht[c * H:(c + 1) * H, :], posh).then_inc(small_in, 16)
                pool.dma_start(ppt[c * H:(c + 1) * H, :], parp[c]).then_inc(small_in, 16)
            for blk in range(NBK):
                s = blk % 2
                pool.wait_ge(evac_a, len(ACT_OUT) * (blk + 1))
                pool.wait_ge(evac_v, len(DVE_OUT) * (blk + 1))
                for k in range(PAD):
                    for dst, src in ((PAD - 1 - k, PAD + 1 + k), (PAD + W + k, PAD + W - 2 - k)):
                        last = pool.tensor_copy(stage[:, s, :, :, dst:dst + 1], stage[:, s, :, :, src:src + 1])
                        if k == PAD - 1:
                            last.then_inc(padded, 1)

        @block.scalar
        def _(act):
            act.wait_ge(fstep, 2)
            act.activation(fold[:, 2:4], fold[:, 0:2], ACT.Sqrt).then_inc(fsqrt, 1)
            act.wait_ge(pstep, 2)
            act.activation(pfold[:, 1:2], pfold[:, 0:1], ACT.Sqrt).then_inc(fsqrt, 1)
            act.wait_ge(gstep, 4)
            act.activation(gstd[:], gvar[:], ACT.Sqrt).then_inc(gsqrt, 1)
            act.wait_ge(pstep, 10)
            for i in range(K7):
                act.activation(feat[:, i, :], ud[:], ACT.Relu, scale=pfold[:, 2:3],
                               bias=vd[:, i:i + 1]).then_inc(feat_done, 1)
            for blk in range(NBK):
                s = blk % 2
                if blk >= 2:
                    act.wait_ge(stored[s], 16 * (3 * (blk // 2) + (2 * PAD if s == 0 else 0)))
                for o in ACT_OUT:
                    act.wait_ge(proj_done, blk * NOUT + o + 1)
                    src = ps[:, (blk * NOUT + o) % 8, 0:CB]
                    if o == 0:
                        act.activation(a1s[:, s, :], src, ACT.Identity, scale=s1c[:], bias=t1c[:]).then_inc(evac_a, 1)
                    elif o == 1:
                        act.activation(stage[:, s, :, SHARE, PAD:PAD + W], src.rearrange("p (h w) -> p h w", w=W),
                                       ACT.Identity, scale=s1c[:], bias=t2c[:]).then_inc(evac_a, 1)
                    else:
                        act.activation(stage[:, s, :, o - 2, PAD:PAD + W], src.rearrange("p (h w) -> p h w", w=W),
                                       ACT.Identity, bias=par[:, B3 + o - 2:B3 + o - 1]).then_inc(evac_a, 1)

        @block.vector
        def _(v):
            v.wait_ge(small_in, N_SMALL)
            v.tensor_scalar(fold[:, 0:1], par[:, V1:V1 + 1], BN_EPS, None, ALU.add).then_inc(fstep, 1)
            v.tensor_scalar(fold[:, 1:2], par[:, V2:V2 + 1], BN_EPS, None, ALU.add).then_inc(fstep, 1)
            v.tensor_scalar(pq[:], pwt[:], ppt[:, WPX:WPX + 1], ppt[:, BP:BP + 1], ALU.mult, ALU.add).then_inc(pstep, 1)
            v.tensor_scalar(pfold[:, 0:1], ppt[:, VP:VP + 1], BN_EPS, None, ALU.add).then_inc(pstep, 1)
            v.tensor_scalar(hq[:], pht[:], ppt[:, WPY:WPY + 1], None, ALU.mult).then_inc(pstep, 1)
            v.wait_ge(pstep, 3)
            v.tensor_tensor(ud[:], pq[:, 0, :], pq[:, 1, :], ALU.subtract).then_inc(pstep, 1)
            v.tensor_scalar(vd[:], hq[:, 1:1 + K7], hq[:, 0:1], -1.0, ALU.subtract, ALU.mult).then_inc(pstep, 1)
            v.wait_ge(fsqrt, 2)
            v.reciprocal(fold[:, 4:6], fold[:, 2:4]).then_inc(fstep, 1)
            v.reciprocal(pfold[:, 2:3], pfold[:, 1:2]).then_inc(pstep, 1)
            v.wait_ge(fstep, 3)
            v.wait_ge(pstep, 6)
            v.tensor_tensor(s1c[:], par[:, G1:G1 + 1], fold[:, 4:5], ALU.mult).then_inc(fstep, 1)
            v.tensor_tensor(s2c[:], par[:, G2:G2 + 1], fold[:, 5:6], ALU.mult).then_inc(fstep, 1)
            v.tensor_tensor(pfold[:, 2:3], ppt[:, GP:GP + 1], pfold[:, 2:3], ALU.mult).then_inc(pstep, 1)
            v.wait_ge(fstep, 5)
            v.wait_ge(pstep, 7)
            v.tensor_scalar(fold[:, 6:7], par[:, B1:B1 + 1], par[:, M1:M1 + 1], s1c[:], ALU.subtract, ALU.mult).then_inc(fstep, 1)
            v.tensor_tensor(t2c[:], par[:, B2:B2 + 1], s1c[:], ALU.mult).then_inc(fstep, 1)
            v.tensor_tensor(fold[:, 7:8], par[:, M2:M2 + 1], s2c[:], ALU.mult).then_inc(fstep, 1)
            v.tensor_scalar(vd[:], vd[:], ppt[:, MP:MP + 1], pfold[:, 2:3], ALU.subtract, ALU.mult).then_inc(pstep, 1)
            v.wait_ge(fstep, 8)
            v.wait_ge(pstep, 8)
            v.tensor_tensor(t1c[:], fold[:, 6:7], par[:, BE1:BE1 + 1], ALU.add).then_inc(fstep, 1)
            v.tensor_tensor(u2c[:], par[:, BE2:BE2 + 1], fold[:, 7:8], ALU.subtract).then_inc(fstep, 1)
            v.tensor_scalar(vd[:], vd[:], ppt[:, BEP:BEP + 1], None, ALU.add).then_inc(pstep, 1)
            v.tensor_copy(cwparts[:, 0, :], cwp[:]).then_inc(parts, 1)
            v.wait_ge(parts, 1)
            v.tensor_tensor(cwp[:], cwp[:], cwparts[:, 0, :], ALU.subtract).then_inc(pstep, 1)
            v.wait_ge(pstep, 10)
            v.tensor_copy(cwparts[:, 1, :], cwp[:]).then_inc(parts, 1)
            v.wait_ge(parts, 2)
            v.tensor_tensor(cwparts[:, 2, :], cwp[:], cwparts[:, 1, :], ALU.subtract).then_inc(parts, 1)

            for n in range(B * CH):
                v.wait_ge(x_in[n], 16)
                for q in range(NBK):
                    v.bn_stats(stats[:, n, q, :], xs[:, n // CH, n % CH, q * CB:(q + 1) * CB]).then_inc(stat_done, 1)
                v.wait_ge(stat_done, NBK * (n + 1))
                v.bn_aggr(mv[:, n, :], stats[:, n]).then_inc(mom_done, 1)
            v.wait_ge(mom_done, B * CH)
            v.tensor_copy(mom[:, 0, :], mv[:, :, 0]).then_inc(gstep, 1)
            v.tensor_tensor(mom[:, 1, :], mv[:, :, 0], mv[:, :, 0], ALU.mult).then_inc(gstep, 1)
            v.wait_ge(gstep, 2)
            v.tensor_tensor(mom[:, 1, :], mom[:, 1, :], mv[:, :, 1], ALU.add).then_inc(mom_done, 1)
            v.wait_ge(gmom_mm, 1)
            v.tensor_copy(gmom[:], ps[:, 0, 0:2 * B * CH].rearrange("p (a n) -> p a n", a=2)).then_inc(mom_done, 1)
            v.wait_ge(mom_done, B * CH + 2)
            v.tensor_tensor(gvar[:], gmom[:, 0, :], gmom[:, 0, :], ALU.mult).then_inc(gstep, 1)
            v.wait_ge(gstep, 3)
            v.scalar_tensor_tensor(gvar[:], gmom[:, 1, :], GN_EPS, gvar[:], ALU.add, ALU.subtract).then_inc(gstep, 1)
            v.wait_ge(gsqrt, 1)
            v.reciprocal(grs[:], gstd[:]).then_inc(gstep, 1)
            v.wait_ge(gstep, 5)
            v.scalar_tensor_tensor(gnb[:], gmom[:, 0, :], -1.0, grs[:], ALU.mult, ALU.mult).then_inc(gstep, 1)
            v.wait_ge(gstep, 6)
            for n in range(B * CH):
                xv = xs[:, n // CH, n % CH, :]
                v.tensor_scalar(xv, xv, grs[:, n:n + 1], gnb[:, n:n + 1], ALU.mult, ALU.add).then_inc(normed, 1)
            v.wait_ge(feat_done, K7)
            v.tensor_copy(fparts[:, 0], feat[:]).then_inc(parts, 1)
            v.wait_ge(parts, 4)
            v.tensor_tensor(feat[:], feat[:], fparts[:, 0], ALU.subtract).then_inc(pstep, 1)
            v.wait_ge(pstep, 11)
            v.tensor_copy(fparts[:, 1], feat[:]).then_inc(parts, 1)
            v.wait_ge(parts, 5)
            v.tensor_tensor(fparts[:, 2], feat[:], fparts[:, 1], ALU.subtract).then_inc(parts, 1)
            for blk in range(NBK):
                s = blk % 2
                if blk >= 2:
                    v.wait_ge(stored[s], 16 * (3 * (blk // 2) + (2 * PAD if s == 0 else 0)))
                for o in DVE_OUT:
                    v.wait_ge(proj_done, blk * NOUT + o + 1)
                    v.tensor_scalar(stage[:, s, :, o - 2, PAD:PAD + W],
                                    ps[:, (blk * NOUT + o) % 8, 0:CB].rearrange("p (h w) -> p h w", w=W),
                                    par[:, B3 + o - 2:B3 + o - 1], None, ALU.add).then_inc(evac_v, 1)

        @block.tensor
        def _(pe):
            pe.wait_ge(small_in, N_SMALL)
            pe.wait_ge(mom_done, B * CH + 1)
            pe.matmul(ps[:, 0, 0:2 * B * CH], gav[:], mom[:].rearrange("p a n -> p (a n)"),
                      start=True, stop=True).then_inc(gmom_mm, 1)
            pe.wait_ge(normed, B * CH)
            pe.wait_ge(mom_done, B * CH + 2)
            for blk in range(NBK):
                for o in range(NOUT):
                    n = blk * NOUT + o
                    if n >= 8:
                        m = n - 8
                        mb, mo = m // NOUT, m % NOUT
                        if mo in DVE_OUT:
                            pe.wait_ge(evac_v, mb * len(DVE_OUT) + DVE_OUT.index(mo) + 1)
                        else:
                            pe.wait_ge(evac_a, mb * len(ACT_OUT) + ACT_OUT.index(mo) + 1)
                    for k in range(CH):
                        for b in range(B):
                            mm = pe.matmul(ps[32 * b:32 * b + 32, n % 8, 0:CB], wts[:, k, o, :],
                                           xs[:, b, k, blk * CB:(blk + 1) * CB], start=(k == 0), stop=(k == CH - 1))
                    mm.then_inc(proj_done, 1)


PAIRS = 10


def tap_units():
    units, t, n = [], 0, TAPS - PAIRS
    made = 0
    while t < TAPS:
        want = (len(units) + 1) * PAIRS // n
        if made < want and t % K7 < K7 - 1:
            units.append((t, t + 1))
            t, made = t + 2, made + 1
        else:
            units.append((t,))
            t += 1
    return units


UNITS = tap_units()
NU = len(UNITS)
NPAIR = sum(len(u) == 2 for u in UNITS)
NPROD = 3
assert NU % NPROD == 0
Z_AT = [max(0, RW * i - 2) for i in range(K7)]
ROW_MAX_AT = [8 + 4 * i for i in range(K7)]
SHIFT_AT = [33, 33, 34, 35, 36, 37, 38]
ROW_SUM_AT = [5 + 3 * i for i in range(K7)]
DEN_AT = 28
CPI = RW
NCH = K7 * CPI
CW = K7 * W


class Blk:

    def __init__(self, it, c):
        self.it, self.c = it, c
        self.n = 2 * it + c
        self.par = c % 2
        self.half = it + c // 2

    def q(self, i):
        return self.n * K7 + i

    def qpar(self, i):
        return (self.c * K7 + i) % 2

    def qhalf(self, i):
        return self.it * K7 + (self.c * K7 + i) // 2 + 1

    def g(self, c):
        return self.n * NCH + c

    def early(self, m):
        return isinstance(self.n, int) and self.n < m


def conv_stage(nc, planes, x2_dram, a1_dram, pf_dram, cw1T, cw2T, ident_dram, conv_dram, keep):
    ctx = ExitStack()
    with ctx:
        def sb(name, shape, dt=F32):
            return ctx.enter_context(nc.sbuf_tensor(name, shape, dt))

        def sem(name):
            return ctx.enter_context(nc.semaphore(name))

        win = [sb(f"win{k}", [P, RW + K7 - 1, SHARE, WP]) for k in range(2)]
        x2w = [sb(f"x2w{k}", [P, RW + K7 - 1, WP]) for k in range(2)]
        a1 = [sb(f"a1w{k}", [P, PW]) for k in range(2)]
        lg = [sb(f"lg{k}", [P, K7, K7, PW]) for k in range(2)]
        y1 = [sb(f"y1{k}", [P, K7, PW]) for k in range(2)]
        y2 = [sb(f"y2{k}", [P, CW]) for k in range(2)]
        prod = [sb(f"prod{k}", [P, SHARE, PW]) for k in range(NPROD)]
        prodb = sb("prodb", [P, SHARE, PW])
        pf = [sb(f"pf{k}", [18, RW, CW], BF16) for k in range(2)]
        osb = sb("osb", [P, SHARE, PW])
        mx = sb("mx", [P, PW])
        rmax = sb("rmax", [P, K7, PW])
        rsum = sb("rsum", [P, K7, PW])
        den = [sb(f"den{k}", [P, PW]) for k in range(2)]
        cw1 = sb("cw1bd", [P, P])
        cw2 = sb("cw2bd", [P, P])
        ident = sb("ident1", [P, P])
        ps = keep["ps"]
        y2p, lgp, acc = ps[:, 0:2], ps[:, 2:4], ps[:, 4:8]
        par, cw1p18, s2c, u2c = (keep[k] for k in ("par", "cw1p18", "s2c", "u2c"))

        wzero = sem("wzero")
        w_in = sem("w_in")
        win_in = [sem(f"win_in{k}") for k in range(2)]
        x_in = [sem(f"x12_in{k}") for k in range(2)]
        pf_in = [sem(f"pf_in{k}") for k in range(2)]
        z_ready = sem("z_ready")
        relu1 = sem("relu1")
        mm1 = sem("mm1")
        relu2 = sem("relu2")
        mm2 = sem("mm2")
        logit = sem("logit")
        maxed = sem("maxed")
        rowmax = sem("rowmax")
        rowsum = sem("rowsum")
        shifted = sem("shifted")
        exped = sem("exped")
        densum = sem("densum")
        rden = sem("rden")
        pairmul = sem("pairmul")
        prod_ready = sem("prod_ready")
        summed = sem("summed")
        outn = sem("outn")
        stored = sem("stored1")

        conv_v = conv_dram.rearrange("b (l s) x -> (b l) s x", s=SHARE)
        block = ctx.enter_context(nc.Block())

        def slots(eng, slot):
            slot(Blk(0, 0), None)
            slot(Blk(0, 1), Blk(0, 0))
            with eng.Fori(0, NW // 2 - 1) as it:
                slot(Blk(it, 2), Blk(it, 1))
                slot(Blk(it, 3), Blk(it, 2))
            slot(None, Blk(0, NW - 1))

        @block.gpsimd
        def _(pool):
            pool.memset(cw1[:], 0.0).then_inc(wzero, 1)
            pool.memset(cw2[:], 0.0).then_inc(wzero, 1)
            pool.wait_ge(wzero, 2)
            for q in range(B):
                r = slice(32 * q, 32 * q + 32)
                pool.dma_start(cw1[r, r], cw1T).then_inc(w_in, 16)
                pool.dma_start(cw2[r, r], cw2T).then_inc(w_in, 16)
            pool.dma_start(ident[:], ident_dram).then_inc(w_in, 16)

            def load(a):
                if not a.early(2):
                    pool.wait_ge(z_ready, a.q(0) - K7)
                pool.dma_start(x2w[a.par][:], x2_dram[:, bass.ds(a.n * RW, RW + K7 - 1)]).then_inc(x_in[a.par], 16)
                pool.dma_start(a1[a.par][:], a1_dram[:, bass.ds(a.n * PW, PW)]).then_inc(x_in[a.par], 16)
                if not a.early(2):
                    pool.wait_ge(prod_ready, NU * (a.n - 1))
                pool.dma_start(win[a.par][:], planes[:, bass.ds(a.n * RW, RW + K7 - 1)]).then_inc(win_in[a.par], 16)

            slots(pool, lambda a, b: a and load(a))

        @block.sync
        def _(sp):
            def store(n):
                if isinstance(n, int) and n < 0:
                    return
                sp.wait_ge(outn, n + 1)
                sp.dma_start(conv_v[:, :, bass.ds(n * PW, PW)], osb[:]).then_inc(stored, 16)

            def slot(a, b):
                if a:
                    for i in range(K7):
                        k = a.qpar(i)
                        if not (a.early(1) and i < 2):
                            sp.wait_ge(mm1, CPI * (a.q(i) - 1))
                        for w in range(3):
                            sp.dma_start(pf[k][6 * w:6 * w + 6], pf_dram[:, i, bass.ds(a.n * RW, RW)]).then_inc(pf_in[k], 16)
                        if b and i == 1:
                            store(b.n - 1)
                elif b:
                    store(b.n - 1)
                if b and not a:
                    store(b.n)

            slots(sp, slot)
            sp.wait_ge(stored, 16 * NW)

        @block.scalar
        def _(act):
            def slot(a, b):
                if not a:
                    return

                def first(i):
                    act.wait_ge(z_ready, a.q(i) + 1)
                    t = y1[a.qpar(i)]
                    act.activation(t[:], t[:], ACT.Relu).then_inc(relu1, 1)

                def second(c):
                    g = a.g(c)
                    act.wait_ge(mm1, g + 1)
                    if not (a.early(1) and c < 2):
                        act.wait_ge(mm2, g - 1)
                    act.activation(y2[c % 2][:], y2p[:, c % 2, 0:CW], ACT.Relu, scale=s2c[:],
                                   bias=u2c[:]).then_inc(relu2, 1)

                def third(c):
                    act.wait_ge(mm2, a.g(c) + 1)
                    if c == 0 and not a.early(2):
                        act.wait_ge(prod_ready, NU * (a.n - 1))
                        act.wait_ge(rowsum, a.q(0) - K7)
                    i, h = c // CPI, c % CPI
                    act.activation(lg[a.par][:, i, :, h * W:(h + 1) * W],
                                   lgp[:, c % 2, 0:CW].rearrange("p (j w) -> p j w", w=W),
                                   ACT.Identity, bias=par[:, CB2:CB2 + 1]).then_inc(logit, 1)

                first(0)
                for c in range(NCH):
                    second(c)
                    if c >= 1:
                        third(c - 1)
                    if c % CPI == CPI - 2 and c // CPI + 1 < K7:
                        first(c // CPI + 1)
                third(NCH - 1)
                for i in range(K7):
                    act.wait_ge(shifted, a.q(i) + 1)
                    act.activation(lg[a.par][:, i], lg[a.par][:, i], ACT.Exp).then_inc(exped, 1)

            act.wait_ge(w_in, 16 * 9)
            slots(act, slot)

        @block.vector
        def _(v):
            def slot(a, b):
                def z(i):
                    q = a.q(i)
                    if i == 0:
                        v.wait_ge(x_in[a.par], 32 * (a.half + 1))
                    if not (a.early(1) and i < 2):
                        v.wait_ge(mm1, CPI * (q - 1))
                    o = y1[a.qpar(i)][:].rearrange("p j (h w) -> p j h w", w=W)
                    x1 = a1[a.par][:].rearrange("p (h w) -> p h w", w=W).unsqueeze(1).broadcast_to([P, K7, RW, W])
                    row = x2w[a.par][:, i:i + RW, 0:W]
                    x2 = bass.AP(row.tensor, row.offset, [row.ap[0], [1, K7], row.ap[1], row.ap[2]])
                    v.tensor_tensor(o, x1, x2, ALU.subtract).then_inc(z_ready, 1)

                def row_max(i):
                    v.wait_ge(logit, a.g(0) + CPI * (i + 1))
                    v.tensor_reduce(rmax[:, i], lg[a.par][:, i].rearrange("p j x -> p x j"), AX.X, ALU.max).then_inc(rowmax, 1)

                def all_max():
                    v.wait_ge(rowmax, a.q(K7))
                    v.tensor_reduce(mx[:], rmax[:].rearrange("p i x -> p x i"), AX.X, ALU.max).then_inc(maxed, 1)

                def shift(i):
                    v.wait_ge(maxed, a.n + 1)
                    l = lg[a.par][:, i]
                    v.tensor_tensor(l, l, mx[:].unsqueeze(1).broadcast_to([P, K7, PW]), ALU.subtract).then_inc(shifted, 1)

                def row_sum(i):
                    v.wait_ge(exped, b.q(i) + 1)
                    v.tensor_reduce(rsum[:, i], lg[b.par][:, i].rearrange("p j x -> p x j"), AX.X, ALU.add).then_inc(rowsum, 1)

                def denominators():
                    v.wait_ge(rowsum, b.q(K7))
                    v.tensor_reduce(den[b.par][:], rsum[:].rearrange("p i x -> p x i"), AX.X, ALU.add).then_inc(densum, 1)
                    v.wait_ge(densum, b.n + 1)
                    v.reciprocal(den[b.par][:], den[b.par][:]).then_inc(rden, 1)

                def mult(t, out):
                    i, j = t // K7, t % K7
                    w = lg[b.par][:, i, j].rearrange("p (h w) -> p h w", w=W).unsqueeze(1).broadcast_to([P, SHARE, RW, W])
                    xw = win[b.par][:, i:i + RW, 0:SHARE, j:j + W].rearrange("p h s w -> p s h w")
                    return v.tensor_tensor(out[:].rearrange("p s (h w) -> p s h w", w=W), w, xw, ALU.mult)

                def unit(u):
                    taps = UNITS[u]
                    if u == 0:
                        v.wait_ge(win_in[b.par], 16 * (b.half + 1))
                    v.wait_ge(exped, b.q(taps[-1] // K7) + 1)
                    if not (b.early(1) and u < NPROD):
                        v.wait_ge(summed, NU * b.n + u + 1 - NPROD)
                    out = prod[u % NPROD]
                    if len(taps) == 1:
                        mult(taps[0], out).then_inc(prod_ready, 1)
                    else:
                        k = sum(len(x) == 2 for x in UNITS[:u])
                        mult(taps[0], out).then_inc(pairmul, 1)
                        mult(taps[1], prodb).then_inc(pairmul, 1)
                        v.wait_ge(pairmul, 2 * (NPAIR * b.n + k + 1))
                        v.tensor_tensor(out[:], out[:], prodb[:], ALU.add).then_inc(prod_ready, 1)

                def normalize(d, n):
                    v.wait_ge(summed, NU * (n + 1))
                    v.wait_ge(rden, n + 1)
                    if not (isinstance(n, int) and n == 0):
                        v.wait_ge(stored, 16 * n)
                    v.tensor_tensor(osb[:].rearrange("p (q t) x -> p q t x", t=2),
                                    acc[:, :, 0:2 * PW].rearrange("p q (t x) -> p q t x", t=2),
                                    d[:].unsqueeze(1).unsqueeze(1).broadcast_to([P, 4, 2, PW]),
                                    ALU.mult).then_inc(outn, 1)

                if not b:
                    for i in range(K7):
                        z(i)
                    for i in range(K7):
                        row_max(i)
                    all_max()
                    for i in range(K7):
                        shift(i)
                    return
                for u in range(NU):
                    for i in range(K7):
                        if a and u == Z_AT[i]:
                            z(i)
                    if a and u in ROW_MAX_AT:
                        row_max(ROW_MAX_AT.index(u))
                    if u == NPROD and not b.early(1):
                        normalize(den[1 - b.par], b.n - 1)
                    if u in ROW_SUM_AT:
                        row_sum(ROW_SUM_AT.index(u))
                    if u == DEN_AT:
                        denominators()
                    if a and u == SHIFT_AT[0]:
                        all_max()
                    for i in range(K7):
                        if a and u == SHIFT_AT[i]:
                            shift(i)
                    unit(u)
                if not a:
                    normalize(den[b.par], b.n)

            slots(v, slot)

        @block.tensor
        def _(pe):
            def slot(a, b):
                def first(c):
                    i, h = c // CPI, c % CPI
                    g = a.g(c)
                    if h == 0:
                        pe.wait_ge(relu1, a.q(i) + 1)
                        pe.wait_ge(pf_in[a.qpar(i)], 48 * a.qhalf(i))
                    if not (a.early(1) and c < 2):
                        pe.wait_ge(relu2, g - 1)
                    out = y2p[:, c % 2, 0:CW]
                    pe.matmul(out.rearrange("p (j w) -> p j w", w=W), cw1[:], y1[a.qpar(i)][:, :, h * W:(h + 1) * W], start=True, stop=False)
                    pe.matmul(out, cw1p18[:], pf[a.qpar(i)][:, h, :], start=False, stop=True).then_inc(mm1, 1)

                def second(c):
                    g = a.g(c)
                    pe.wait_ge(relu2, g + 1)
                    if not (a.early(1) and c < 2):
                        pe.wait_ge(logit, g - 1)
                    pe.matmul(lgp[:, c % 2, 0:CW], cw2[:], y2[c % 2][:], start=True, stop=True).then_inc(mm2, 1)

                def unit(u):
                    pe.wait_ge(prod_ready, NU * b.n + u + 1)
                    if u == 0 and not b.early(1):
                        pe.wait_ge(outn, b.n)
                    for q in range(4):
                        mm = pe.matmul(acc[:, q, 0:2 * PW], ident[:], prod[u % NPROD][:, 2 * q:2 * q + 2, :].rearrange("p s x -> p (s x)"),
                                       start=(u == 0), stop=(u == NU - 1))
                    mm.then_inc(summed, 1)

                if not b:
                    for c in range(NCH + 1):
                        if c < NCH:
                            first(c)
                        if c >= 1:
                            second(c - 1)
                    return
                for u in range(NU):
                    if a and u < NCH:
                        first(u)
                    if a and 1 <= u < 1 + NCH:
                        second(u - 1)
                    unit(u)

            pe.wait_ge(w_in, 16 * 9)
            slots(pe, slot)



CT = 448
NCT = S // CT
HEADS, DH = 8, 32
HG = 2
HPG = HEADS // HG
NT = -(-S // P)
SCALE = DH ** -0.5
SHIFT = 5.0
ROT = DH // 2 + 1
NFK = ROT * DH + DH + 2
KH = ((0, 9 * DH), (9 * DH, NFK))
KX = DH + DH // 2
FLIN, FONE = ROT * DH, ROT * DH + DH
FT = 5
LASTK = 3 * DH + 1
HID = 4 * C
HT = HID // P
TOPK = S // 2 - 1
LN_EPS = 1e-5


def tile_rows(j):
    return min(P, S - j * P)


class Norm:

    def __init__(self, ctx, nc, tag, t, xn, avg, eps, banks):
        def sb(name, shape):
            return ctx.enter_context(nc.sbuf_tensor(name + tag, shape, F32))

        def sem(name):
            return ctx.enter_context(nc.semaphore(name + tag))

        self.t, self.xn, self.avg, self.eps, self.banks = t, xn, avg, eps, banks
        self.sq = [sb(f"lsq{k}", [P, CH, CT]) for k in range(2)]
        self.m2 = [sb(f"lm2{k}", [P, CT]) for k in range(2)]
        self.var = [sb(f"lvar{k}", [P, CT]) for k in range(2)]
        self.s_sq_done = sem("s_sq_done")
        self.s_stat = sem("s_stat")
        self.s_m2_done = sem("s_m2_done")
        self.s_var_done = sem("s_var_done")
        self.s_std_done = sem("s_std_done")
        self.s_rstd = sem("s_rstd")
        self.s_cent = sem("s_cent")
        self.s_xn_done = sem("s_xn_done")

    def ch(self, c):
        return slice(c * CT, (c + 1) * CT)

    def act(self, act, b, ready):
        def square(c):
            ready(c)
            if c >= 2:
                act.wait_ge(self.s_stat, b * NCT + c - 1)
            act.activation(self.sq[c % 2][:], self.t[:, :, self.ch(c)], ACT.Square).then_inc(self.s_sq_done, 1)

        def mean2(c):
            act.wait_ge(self.s_stat, b * NCT + c + 1)
            act.activation(self.m2[c % 2][:], self.banks[:, 2 * (c % 2), 0:CT], ACT.Square).then_inc(self.s_m2_done, 1)

        def std(c):
            act.wait_ge(self.s_var_done, b * NCT + c + 1)
            v = self.var[c % 2][:]
            act.activation(v, v, ACT.Sqrt, bias=self.eps[:]).then_inc(self.s_std_done, 1)

        square(0)
        square(1)
        for c in range(NCT):
            mean2(c)
            if c + 2 < NCT:
                square(c + 2)
            if c >= 1:
                std(c - 1)
        std(NCT - 1)

    def pe(self, pe, b, ready):
        for c in range(NCT):
            ready(c)
            if c >= 2:
                pe.wait_ge(self.s_var_done, b * NCT + c - 1)
                pe.wait_ge(self.s_cent, b * NCT + c - 1)
            pe.wait_ge(self.s_sq_done, b * NCT + c + 1)
            for k in range(CH):
                pe.matmul(self.banks[:, 2 * (c % 2), 0:CT], self.avg[:], self.t[:, k, self.ch(c)],
                          start=(k == 0), stop=(k == CH - 1))
            for k in range(CH):
                mm = pe.matmul(self.banks[:, 2 * (c % 2) + 1, 0:CT], self.avg[:], self.sq[c % 2][:, k, :],
                               start=(k == 0), stop=(k == CH - 1))
            mm.then_inc(self.s_stat, 1)

    def dve(self, v, b):
        def variance(c):
            v.wait_ge(self.s_m2_done, b * NCT + c + 1)
            if c >= 2:
                v.wait_ge(self.s_xn_done, b * NCT + c - 1)
            v.tensor_tensor(self.var[c % 2][:], self.banks[:, 2 * (c % 2) + 1, 0:CT], self.m2[c % 2][:],
                            ALU.subtract).then_inc(self.s_var_done, 1)
            o = self.xn[:, :, self.ch(c)]
            v.tensor_tensor(o, self.t[:, :, self.ch(c)],
                            self.banks[:, 2 * (c % 2), 0:CT].unsqueeze(1).broadcast_to([P, CH, CT]),
                            ALU.subtract).then_inc(self.s_cent, 1)

        def scale(c):
            v.wait_ge(self.s_std_done, b * NCT + c + 1)
            r = self.var[c % 2]
            v.reciprocal(r[:], r[:]).then_inc(self.s_rstd, 1)
            v.wait_ge(self.s_rstd, b * NCT + c + 1)
            v.wait_ge(self.s_cent, b * NCT + c + 1)
            o = self.xn[:, :, self.ch(c)]
            v.tensor_tensor(o, o, r[:].unsqueeze(1).broadcast_to([P, CH, CT]), ALU.mult).then_inc(self.s_xn_done, 1)

        for c in range(NCT):
            variance(c)
            if c >= 1:
                scale(c - 1)
        scale(NCT - 1)


def attention_stage(nc, x, conv_dram, t2_dram, wq, wkv, bkv, bq, projw, projb, sel_dram, selb_dram, heads_dram,
                    avg_dram, ident_dram, keep):
    ctx = ExitStack()
    with ctx:
        def sb(name, shape, dt=F32):
            return ctx.enter_context(nc.sbuf_tensor(name, shape, dt))

        def sem(name):
            return ctx.enter_context(nc.semaphore(name))

        ps = keep["ps"]
        t = sb("t", [P, CH, S])
        xn = sb("xn", [P, CH, S])
        qsp = sb("qsp", [P, 3, S], BF16)
        qst = sb("qst", [3 * DH, HPG, S], BF16)
        at = sb("at", [P, HG, S])
        wq_s = sb("wq_s", [P, CH, HG, P])
        wkv_s = sb("wkv_s", [P, CH, HG, HPG * KX + P])
        bkv_s = sb("bkv_s", [P, HG, HPG * KX + P])
        bq_s = sb("bq_s", [P, HG])
        pw_s = sb("pw_s", [P, HG, C])
        pb_s = sb("pb_s", [P, CH])
        self32 = sb("self32", [3 * DH, FT, P])
        sel = sb("sel", [3 * DH, FT, P], BF16)
        selb = sb("selb", [P, 1])
        avg = sb("avg", [P, P])
        ident = sb("ident2", [P, P])
        heads = sb("heads", [P, P])
        nkeys = sb("nkeys", [P, 1])
        eps = sb("eps", [P, 1])
        kv = [sb(f"kv{k}", [P, HPG * KX + P]) for k in range(3)]
        phk = [sb(f"phk{k}", [P, HPG, NFK]) for k in range(2)]
        sn = sb("sn", [P, FT * P])
        sx = sb("sx", [P, ROT - 2, 2, DH])
        corr = [sb(f"corr{k}", [P, DH]) for k in range(3)]
        snt = sb("snt", [P, FT, P])
        gram = sb("gram", [P, HPG, DH])
        kbar = sb("kbar", [P, 1])
        qr = [sb(f"qr{k}", [P, CT]) for k in range(2)]
        phq = [sb(f"phq{k}", [P, HPG, CT]) for k in range(2)]
        qt = [sb(f"qt{k}", [P, CT]) for k in range(2)]
        rd = [sb(f"rd{k}", [P, CT]) for k in range(2)]
        norm = Norm(ctx, nc, "a", t, xn, avg, eps, ps[:, 0:4])

        w_in = sem("w_in2")
        ready0 = sem("ready0")
        sel_ready = sem("sel_ready")
        gate = sem("gate2")
        x_in = [sem(f"x_in2{c}") for c in range(NCT)]
        conv_in = sem("conv_in")
        t2_out = [sem(f"t2_out{c}") for c in range(NCT)]
        tsum = sem("tsum")
        names = ("q_mm qf_done qh_done qr_done qm_done ql_done qst_in kv_mm kv_done klin "
                 "phi s_mm sn_done cor gram_done tr snt_done sel_mm phq_done o_mm t_mm qt_done den_mm den_done rd_done att p_mm t2_done")
        m = {n: sem(n) for n in names.split()}
        q_mm, qf_done, qh_done, qr_done, qm_done, ql_done, qst_in, kv_mm, kv_done, klin, phi, s_mm, sn_done, cor, \
            gram_done, tr, snt_done, sel_mm, phq_done, o_mm, t_mm, qt_done, den_mm, den_done, rd_done, att, p_mm, t2_done = \
            (m[n] for n in names.split())
        x_v = x.rearrange("b (k p) s -> b p k s", p=P)
        conv_v = conv_dram.rearrange("b (k p) s -> b p k s", p=P)
        t2_v = t2_dram.rearrange("b (k p) s -> b p k s", p=P)
        NSN = 8
        NSEL = NCT * FT * 2

        def ch(c):
            return slice(c * CT, (c + 1) * CT)

        block = ctx.enter_context(nc.Block())

        @block.gpsimd
        def _(pool):
            for out, src in ((wq_s, wq), (wkv_s, wkv), (bkv_s, bkv), (bq_s, bq), (pw_s, projw), (pb_s, projb),
                             (self32, sel_dram), (selb, selb_dram), (heads, heads_dram), (avg, avg_dram), (ident, ident_dram)):
                pool.dma_start(out[:], src).then_inc(w_in, 16)
            pool.memset(nkeys[:], SHIFT * SHIFT * S).then_inc(ready0, 1)
            pool.memset(eps[:], LN_EPS).then_inc(ready0, 1)
            for k in range(2):
                pool.memset(phk[k][:, :, FONE:FONE + 1], 1.0).then_inc(ready0, 1)
                pool.memset(phk[k][:, :, FONE + 1:NFK], 0.0).then_inc(ready0, 1)
        NW_IN = 16 * 11

        @block.sync
        def _(sp):
            def load_conv(b):
                sp.dma_start(xn[:], conv_v[bass.ds(b, 1)]).then_inc(conv_in, 16)

            def stack(b):
                for hg in range(HG):
                    sp.wait_ge(ql_done, b * HG * NCT + (hg + 1) * NCT)
                    sp.wait_ge(qm_done, b * HG * NCT + (hg + 1) * NCT)
                    if hg > 0:
                        sp.wait_ge(sel_mm, b * HG * NSEL + NSEL)
                    for f in range(3):
                        for h in range(HPG):
                            sp.dma_start(qst[32 * f:32 * f + 32, h, :], qsp[32 * h:32 * h + 32, f, :]).then_inc(qst_in, 16)

            def store(b, c):
                sp.wait_ge(t2_done, b * NCT * CH + (c + 1) * CH)
                sp.dma_start(t2_v[bass.ds(b, 1), :, :, ch(c)], t[:, :, ch(c)]).then_inc(t2_out[c], 16)

            for c in range(NCT):
                sp.dma_start(t[:, :, ch(c)], x_v[0, :, :, ch(c)]).then_inc(x_in[c], 16)
            load_conv(0)
            with sp.Fori(0, B - 1) as b:
                stack(b)
                sp.wait_ge(kv_mm, (b + 1) * HG * NT)
                load_conv(b + 1)
                for c in range(NCT):
                    store(b, c)
                for c in range(NCT):
                    sp.wait_ge(t2_out[c], 16 * (b + 1))
                    sp.dma_start(t[:, :, ch(c)], x_v[bass.ds(b + 1, 1), :, :, ch(c)]).then_inc(x_in[c], 16)
            stack(B - 1)
            for c in range(NCT):
                store(B - 1, c)
            for c in range(NCT):
                sp.wait_ge(t2_out[c], 16 * B)

        @block.scalar
        def _(act):
            def queries(b, hg):
                for c in range(NCT):
                    n = b * HG * NCT + hg * NCT + c
                    bank = ps[:, 6 + c % 2, 0:CT]
                    act.wait_ge(q_mm, n + 1)
                    if hg > 0 and c == 0:
                        act.wait_ge(qst_in, 16 * (b * HG * 3 * HPG + 3 * HPG))
                    act.activation(at[:, hg, ch(c)], bank, ACT.Identity, bias=bq_s[:, hg:hg + 1]).then_inc(qf_done, 1)
                    act.activation(qsp[:, 0, ch(c)], bank, ACT.Identity, bias=bq_s[:, hg:hg + 1]).then_inc(qh_done, 1)
                    if c >= 1:
                        middle(b, hg, c - 1)
                middle(b, hg, NCT - 1)

            def middle(b, hg, c):
                act.wait_ge(qr_done, b * HG * NCT + hg * NCT + c + 1)
                act.activation(qsp[:, 1, ch(c)], qr[c % 2][:], ACT.Copy).then_inc(qm_done, 1)

            def keys(b, hg):
                for j in range(NT):
                    n = b * HG * NT + hg * NT + j
                    r = tile_rows(j)
                    act.wait_ge(kv_done, n + 1)
                    if j >= 2:
                        act.wait_ge(s_mm, n - 1)
                    act.activation(phk[j % 2][0:r, :, FLIN:FLIN + DH],
                                   kv[j % 3][0:r, 0:HPG * KX].rearrange("p (h i) -> p h i", i=KX)[:, :, 0:DH],
                                   ACT.Copy).then_inc(klin, 1)

            def sums(b, hg):
                act.wait_ge(s_mm, b * HG * NT + (hg + 1) * NT)
                s2, s1 = SCALE * SCALE, 2 * SHIFT * SCALE / 4
                lo, hi = ps[:, 0, :], ps[:, 1, :]
                f0 = KH[1][0]
                r16, lin, one = 4 * P - f0, FLIN - f0, FONE - f0
                for dst, width, src, f in (
                    (0, f0, lo[:, 0:f0], s2),
                    (f0, r16, hi[:, 0:r16], s2),
                    (4 * P, DH, hi[:, r16:r16 + DH], s2 / 2),
                    (4 * P + DH, DH, hi[:, lin:lin + DH], s1),
                    (4 * P + 2 * DH, DH, hi[:, lin:lin + DH], -s1),
                    (4 * P + 3 * DH, 1, hi[:, one:one + 1], SHIFT * SHIFT),
                ):
                    act.activation(sn[:, dst:dst + width], src, ACT.Copy, scale=f).then_inc(sn_done, 1)
                for r0, n, src in ((0, 8, lo[:, DH:f0]), (8, 7, hi[:, 0:r16])):
                    act.activation(sx[:, r0:r0 + n], src.rearrange("p (r i) -> p r i", i=DH).unsqueeze(2).broadcast_to([P, n, 2, DH]),
                                   ACT.Copy, scale=s2).then_inc(sn_done, 1)

            def squares(b, hg):
                for c in range(NCT):
                    for f in range(FT):
                        for hp in range(2):
                            n = (c * FT + f) * 2 + hp
                            act.wait_ge(sel_mm, b * HG * NSEL + hg * NSEL + n + 1)
                            k = c * FT + f
                            if k >= 2 and hp == 0:
                                act.wait_ge(o_mm, b * HG * NCT * FT + hg * NCT * FT + k - 1)
                            src = ps[:, 2 * hp:2 * hp + 2, 0:CT]
                            dst = phq[k % 2][:, 2 * hp:2 * hp + 2, :]
                            if f < FT - 1:
                                act.activation(dst, src, ACT.Square).then_inc(phq_done, 1)
                            else:
                                act.activation(dst, src, ACT.Square, bias=selb[:]).then_inc(phq_done, 1)
                        if f == FT - 2:
                            n = b * HG * NCT + hg * NCT + c
                            act.wait_ge(den_mm, n + 1)
                            if c >= 2:
                                act.wait_ge(att, n - 1)
                            act.activation(rd[c % 2][:], ps[:, 7, 0:CT], ACT.Identity, bias=nkeys[:]).then_inc(den_done, 1)

            act.wait_ge(ready0, 6)
            act.wait_ge(w_in, NW_IN)
            with act.Fori(0, B) as b:
                norm.act(act, b, lambda c: act.wait_ge(tsum, b * NCT + c + 1))
                for hg in range(HG):
                    queries(b, hg)
                    keys(b, hg)
                    sums(b, hg)
                    squares(b, hg)

        @block.vector
        def _(v):
            v.wait_ge(w_in, NW_IN)
            v.wait_ge(ready0, 6)
            v.tensor_copy(sel[:], self32[:]).then_inc(sel_ready, 1)

            def queries(b, hg):
                def low(c):
                    v.wait_ge(qm_done, b * HG * NCT + hg * NCT + c + 1)
                    v.tensor_tensor(qsp[:, 2, ch(c)], qr[c % 2][:], qsp[:, 1, ch(c)], ALU.subtract).then_inc(ql_done, 1)
                for c in range(NCT):
                    v.wait_ge(qh_done, b * HG * NCT + hg * NCT + c + 1)
                    if c >= 2:
                        v.wait_ge(ql_done, b * HG * NCT + hg * NCT + c - 1)
                    v.tensor_tensor(qr[c % 2][:], at[:, hg, ch(c)], qsp[:, 0, ch(c)], ALU.subtract).then_inc(qr_done, 1)
                    low(c)

            def keys(b, hg):
                def evacuate(j):
                    n = b * HG * NT + hg * NT + j
                    r = tile_rows(j)
                    v.wait_ge(kv_mm, n + 1)
                    if j >= 3:
                        v.wait_ge(s_mm, n - 2)
                        v.wait_ge(klin, n - 2)
                    v.tensor_tensor(kv[j % 3][0:r, :], ps[0:r, 4 + j % 2, 0:HPG * KX + P], bkv_s[0:r, hg, :],
                                    ALU.add).then_inc(kv_done, 1)

                evacuate(0)
                for j in range(NT):
                    n = b * HG * NT + hg * NT + j
                    r = tile_rows(j)
                    if j + 1 < NT:
                        evacuate(j + 1)
                    ki = kv[j % 3][0:r, 0:HPG * KX].rearrange("p (h i) -> p h i", i=KX)[:, :, 0:DH]
                    v.wait_ge(kv_done, n + 1)
                    if j >= 2:
                        v.wait_ge(s_mm, n - 1)
                    kr = bass.AP(ki.tensor, ki.offset, [ki.ap[0], ki.ap[1], [1, ROT], [1, DH]])
                    v.tensor_tensor(phk[j % 2][0:r, :, 0:FLIN].rearrange("p h (r i) -> p h r i", i=DH),
                                    ki.unsqueeze(2).broadcast_to([r, HPG, ROT, DH]), kr, ALU.mult).then_inc(phi, 1)

            def corrections(b, hg):
                m = b * HG + hg
                v.wait_ge(s_mm, (m + 1) * NT)
                v.scalar_tensor_tensor(gram[:], ps[:, 2, 0:DH].unsqueeze(1).broadcast_to([P, HPG, DH]),
                                       SCALE * SCALE, heads[:].rearrange("p (h i) -> p h i", i=DH),
                                       ALU.mult, ALU.mult).then_inc(gram_done, 1)
                v.tensor_scalar(kbar[:], ps[:, 2, DH:DH + 1], 2 * SHIFT * SCALE, None, ALU.mult).then_inc(gram_done, 1)
                v.wait_ge(sn_done, NSN * (m + 1))
                v.tensor_reduce(corr[0][:], sn[:, DH:4 * P].rearrange("p (r i) -> p i r", i=DH), AX.X, ALU.add).then_inc(cor, 1)
                a = sx[:]
                back = bass.AP(a.tensor, a.offset + DH - 1, [a.ap[0], [1, DH], [2 * DH - 1, ROT - 2]])
                v.tensor_reduce(corr[1][:], back, AX.X, ALU.add).then_inc(cor, 1)
                v.scalar_tensor_tensor(corr[2][:], sn[:, 4 * P:4 * P + DH], -2.0, sn[:, 0:DH], ALU.mult, ALU.add).then_inc(cor, 1)
                v.wait_ge(cor, 5 * m + 3)
                v.tensor_tensor(corr[0][:], corr[0][:], corr[1][:], ALU.add).then_inc(cor, 1)
                v.wait_ge(cor, 5 * m + 4)
                v.tensor_tensor(sn[:, 0:DH], corr[2][:], corr[0][:], ALU.subtract).then_inc(cor, 1)

            def turned(b, hg):
                m = b * HG + hg
                v.wait_ge(tr, 2 * m + 2)
                v.tensor_copy(snt[:, 0:4, :], ps[:, 4, :].rearrange("p (f m) -> p f m", m=P)).then_inc(snt_done, 1)
                v.tensor_copy(snt[0:LASTK, 4, :], ps[0:LASTK, 6, 0:P]).then_inc(snt_done, 1)

            def outputs(b, hg):
                def weigh(c):
                    n = b * HG * NCT + hg * NCT + c
                    v.wait_ge(t_mm, n + 1)
                    if c >= 2:
                        v.wait_ge(den_mm, n - 1)
                    v.scalar_tensor_tensor(qt[c % 2][:], ps[:, 6, 0:CT], kbar[:], at[:, hg, ch(c)], ALU.add, ALU.mult).then_inc(qt_done, 1)

                v.wait_ge(gram_done, 2 * (b * HG + hg) + 2)
                weigh(0)
                for c in range(NCT):
                    n = b * HG * NCT + hg * NCT + c
                    v.wait_ge(den_done, n + 1)
                    v.reciprocal(rd[c % 2][:], rd[c % 2][:]).then_inc(rd_done, 1)
                    if c + 1 < NCT:
                        weigh(c + 1)
                    v.wait_ge(rd_done, n + 1)
                    v.wait_ge(qt_done, n + 1)
                    v.wait_ge(o_mm, b * HG * NCT * FT + hg * NCT * FT + (c + 1) * FT)
                    v.tensor_tensor(at[:, hg, ch(c)], ps[:, 4 + c % 2, 0:CT], rd[c % 2][:], ALU.mult).then_inc(att, 1)

            with v.Fori(0, B) as b:
                v.wait_ge(conv_in, 16 * (b + 1))
                for c in range(NCT):
                    v.wait_ge(x_in[c], 16 * (b + 1))
                    v.tensor_tensor(t[:, :, ch(c)], t[:, :, ch(c)], xn[:, :, ch(c)], ALU.add).then_inc(tsum, 1)
                norm.dve(v, b)
                for hg in range(HG):
                    queries(b, hg)
                    keys(b, hg)
                    corrections(b, hg)
                    turned(b, hg)
                    outputs(b, hg)
                for c in range(NCT):
                    for h in range(CH):
                        n = c * CH + h
                        v.wait_ge(p_mm, b * NCT * CH + n + 1)
                        o = t[:, h, ch(c)]
                        v.scalar_tensor_tensor(o, ps[:, n % 4, 0:CT], pb_s[:, h:h + 1], o, ALU.add, ALU.add).then_inc(t2_done, 1)

        @block.tensor
        def _(pe):
            def queries(b, hg):
                for c in range(NCT):
                    n = b * HG * NCT + hg * NCT + c
                    if hg == 0:
                        pe.wait_ge(norm.s_xn_done, b * NCT + c + 1)
                    if c >= 2:
                        pe.wait_ge(qh_done, n - 1)
                    for k in range(CH):
                        mm = pe.matmul(ps[:, 6 + c % 2, 0:CT], wq_s[:, k, hg, :], xn[:, k, ch(c)], start=(k == 0), stop=(k == CH - 1))
                    mm.then_inc(q_mm, 1)

            def keys(b, hg):
                def project(j):
                    n = b * HG * NT + hg * NT + j
                    r = tile_rows(j)
                    if j >= 2:
                        pe.wait_ge(kv_done, n - 1)
                    for k in range(CH):
                        mm = pe.matmul(ps[0:r, 4 + j % 2, 0:HPG * KX + P], xn[:, k, j * P:j * P + r], wkv_s[:, k, hg, :],
                                       start=(k == 0), stop=(k == CH - 1))
                    mm.then_inc(kv_mm, 1)

                project(0)
                project(1)
                for j in range(NT):
                    n = b * HG * NT + hg * NT + j
                    r = tile_rows(j)
                    if j + 2 < NT:
                        project(j + 2)
                    pe.wait_ge(klin, n + 1)
                    pe.wait_ge(phi, n + 1)
                    if r < P:
                        pe.sem_inc(gate, 1)
                    for f, (lo, hi) in enumerate(KH):
                        for h in range(HPG):
                            v0 = HPG * KX + DH * h
                            pe.matmul(ps[DH * h:DH * h + DH, f, 0:hi - lo], kv[j % 3][0:r, v0:v0 + DH],
                                      phk[j % 2][0:r, h, lo:hi], start=(j == 0), stop=(j == NT - 1))
                    for h in range(HPG):
                        mm = pe.matmul(ps[DH * h:DH * h + DH, 2, 0:DH + 1], kv[j % 3][0:r, KX * h:KX * h + DH],
                                       phk[j % 2][0:r, h, FLIN:FLIN + DH + 1], start=(j == 0), stop=(j == NT - 1))
                    mm.then_inc(s_mm, 1)

            def turn(b, hg):
                pe.wait_ge(cor, 5 * (b * HG + hg) + 5)
                for f in range(4):
                    mm = pe.transpose(ps[:, 4, f * P:(f + 1) * P], sn[:, f * P:(f + 1) * P], ident[:])
                mm.then_inc(tr, 1)
                pe.transpose(ps[0:LASTK, 6, 0:P], sn[:, 4 * P:4 * P + LASTK], ident[:]).then_inc(tr, 1)

            def outputs(b, hg):
                def select(n):
                    k, hp = n // 2, n % 2
                    c, f = k // FT, k % FT
                    if n >= 2:
                        pe.wait_ge(phq_done, b * HG * NSEL + hg * NSEL + n - 1)
                    for h in (2 * hp, 2 * hp + 1):
                        mm = pe.matmul(ps[:, h, 0:CT], sel[:, f, :], qst[:, h, ch(c)], start=True, stop=True)
                    mm.then_inc(sel_mm, 1)

                pe.wait_ge(qst_in, 16 * 3 * HPG * (b * HG + hg + 1))
                pe.wait_ge(snt_done, 2 * (b * HG + hg + 1))
                pe.wait_ge(gram_done, 2 * (b * HG + hg + 1))
                def gram_q(c):
                    n = b * HG * NCT + hg * NCT + c
                    if c >= 1:
                        pe.wait_ge(qt_done, n)
                    pe.matmul(ps[:, 6, 0:CT], gram[:].rearrange("p h i -> p (h i)"), at[:, hg, ch(c)], start=True, stop=True).then_inc(t_mm, 1)

                select(0)
                select(1)
                gram_q(0)
                for k in range(NCT * FT):
                    c, f = k // FT, k % FT
                    if k + 1 < NCT * FT:
                        select(2 * k + 2)
                        select(2 * k + 3)
                    pe.wait_ge(phq_done, b * HG * NSEL + hg * NSEL + 2 * k + 2)
                    if f == 0 and c >= 2:
                        pe.wait_ge(att, b * HG * NCT + hg * NCT + c - 1)
                    kr = P if f < FT - 1 else LASTK
                    for h in range(HPG):
                        mm = pe.matmul(ps[DH * h:DH * h + DH, 4 + c % 2, 0:CT], snt[0:kr, f, DH * h:DH * h + DH],
                                       phq[k % 2][0:kr, h, :], start=(f == 0), stop=(f == FT - 1))
                    mm.then_inc(o_mm, 1)
                    n = b * HG * NCT + hg * NCT + c
                    if f == 2:
                        pe.wait_ge(qt_done, n + 1)
                        if c >= 1:
                            pe.wait_ge(den_done, n)
                        pe.matmul(ps[:, 7, 0:CT], heads[:], qt[c % 2][:], start=True, stop=True).then_inc(den_mm, 1)
                        if c + 1 < NCT:
                            gram_q(c + 1)

            pe.wait_ge(w_in, NW_IN)
            pe.wait_ge(ready0, 6)
            pe.wait_ge(sel_ready, 1)
            with pe.Fori(0, B) as b:
                norm.pe(pe, b, lambda c: pe.wait_ge(tsum, b * NCT + c + 1))
                for hg in range(HG):
                    if hg > 0:
                        pe.wait_ge(att, b * HG * NCT + NCT)
                    queries(b, hg)
                    keys(b, hg)
                    turn(b, hg)
                    outputs(b, hg)
                for c in range(NCT):
                    for h in range(CH):
                        n = c * CH + h
                        pe.wait_ge(att, b * HG * NCT + NCT + c + 1)
                        if n >= 4:
                            pe.wait_ge(t2_done, b * NCT * CH + n - 3)
                        for k in range(HG):
                            mm = pe.matmul(ps[:, n % 4, 0:CT], pw_s[:, k, h * P:(h + 1) * P], at[:, k, ch(c)],
                                           start=(k == 0), stop=(k == HG - 1))
                        mm.then_inc(p_mm, 1)


def routed_stage(nc, t2_dram, out, wr, br, w1, b1, w2, b2, avg_dram, ident_dram, tri_dram, keep):
    ctx = ExitStack()
    with ctx:
        def sb(name, shape, dt=F32):
            return ctx.enter_context(nc.sbuf_tensor(name, shape, dt))

        def sem(name):
            return ctx.enter_context(nc.semaphore(name))

        ps = keep["ps"]
        t = sb("t3", [P, CH, S])
        xn = sb("xn3", [P, CH, S])
        wrow = sb("wrow", [P, S])
        wcol = sb("wcol", [P, NT])
        beats = [sb(f"beats{k}", [P, S], BF16) for k in range(2)]
        ties = [sb(f"ties{k}", [P, P]) for k in range(2)]
        ybuf = [sb(f"ybuf{k}", [P, CT]) for k in range(CH)]
        hid = [sb(f"hid{k}", [P, HT, CT]) for k in range(2)]
        w1_s = sb("w1_s", [P, CH, HID])
        w2_s = sb("w2_s", [P, HT, C])
        b1_s = sb("b1_s", [P, HT])
        b2_s = sb("b2_s", [P, CH])
        wr_s = sb("wr_s", [P, CH])
        wrb = sb("wrb", [P, CH, P])
        br_s = sb("br_s", [P, 1])
        avg = sb("avg3", [P, P])
        ident = sb("ident3", [P, P])
        tri = sb("tri", [P, P])
        ones = sb("ones3", [P, P], BF16)
        eps = sb("eps3", [P, 1])
        norm = Norm(ctx, nc, "f", t, xn, avg, eps, ps[:, 0:4])

        w_in = sem("w_in3")
        ready0 = sem("ready3")
        wrb_ready = sem("wrb_ready")
        gate = sem("gate3")
        t_in = [sem(f"t_in{c}") for c in range(NCT)]
        out_st = [sem(f"out_st{c}") for c in range(NCT)]
        r_mm, r_done, wc_mm, wc_done, bt_lt, bt_le, bt_tie, bt_done, rk_mm, mw, up_mm, gelu, dn_mm, ysc, yxn, fin = (
            sem(n) for n in "r_mm r_done wc_mm wc_done bt_lt bt_le bt_tie bt_done rk_mm mw up_mm gelu dn_mm ysc yxn fin".split())
        t2_v = t2_dram.rearrange("b (k p) s -> b p k s", p=P)
        out_v = out.rearrange("b (k p) s -> b p k s", p=P)

        def ch(c):
            return slice(c * CT, (c + 1) * CT)

        block = ctx.enter_context(nc.Block())

        @block.gpsimd
        def _(pool):
            for o, src in ((w1_s, w1), (w2_s, w2), (b1_s, b1), (b2_s, b2), (wr_s, wr), (br_s, br),
                           (avg, avg_dram), (ident, ident_dram), (tri, tri_dram)):
                pool.dma_start(o[:], src).then_inc(w_in, 16)
            pool.memset(ones[:], 1.0).then_inc(ready0, 1)
            pool.memset(eps[:], LN_EPS).then_inc(ready0, 1)
        NW_IN = 16 * 9

        @block.sync
        def _(sp):
            def store(b, c):
                sp.wait_ge(fin, b * NCT * CH + (c + 1) * CH)
                sp.dma_start(out_v[bass.ds(b, 1), :, :, ch(c)], t[:, :, ch(c)]).then_inc(out_st[c], 16)

            def load(b, c):
                sp.dma_start(t[:, :, ch(c)], t2_v[bass.ds(b, 1), :, :, ch(c)]).then_inc(t_in[c], 16)

            for c in range(NCT):
                load(0, c)
            with sp.Fori(0, B - 1) as b:
                for c in range(NCT):
                    store(b, c)
                for c in range(NCT):
                    sp.wait_ge(out_st[c], 16 * (b + 1))
                    load(b + 1, c)
            for c in range(NCT):
                store(B - 1, c)
            for c in range(NCT):
                sp.wait_ge(out_st[c], 16 * B)

        @block.scalar
        def _(act):
            act.wait_ge(w_in, NW_IN)
            act.wait_ge(ready0, 2)
            with act.Fori(0, B) as b:
                norm.act(act, b, lambda c: act.wait_ge(t_in[c], 16 * (b + 1)))
                for c in range(NCT):
                    act.wait_ge(r_mm, b * NCT + c + 1)
                    act.activation(wrow[:, ch(c)], ps[:, 4 + c % 2, 0:CT], ACT.Identity, bias=br_s[:]).then_inc(r_done, 1)
                for c in range(NCT):
                    for h in range(HT):
                        n = c * HT + h
                        act.wait_ge(up_mm, b * NCT * HT + n + 1)
                        if c >= 2 and h == 0:
                            act.wait_ge(dn_mm, b * NCT * CH + (c - 1) * CH)
                        act.activation(hid[c % 2][:, h, :], ps[:, n % 4, 0:CT], ACT.Gelu_apprx_tanh,
                                       bias=b1_s[:, h:h + 1]).then_inc(gelu, 1)

        @block.vector
        def _(v):
            v.wait_ge(w_in, NW_IN)
            v.wait_ge(ready0, 2)
            v.tensor_copy(wrb[:], wr_s[:].unsqueeze(2).broadcast_to([P, CH, P])).then_inc(wrb_ready, 1)
            with v.Fori(0, B) as b:
                norm.dve(v, b)
                v.wait_ge(wc_mm, b + 1)
                v.tensor_copy(wcol[:, 0:NT - 1], ps[:, 7, 0:NT - 1]).then_inc(wc_done, 1)
                rl = tile_rows(NT - 1)
                v.tensor_copy(wcol[0:rl, NT - 1:NT], ps[0:rl, 7, NT - 1:NT]).then_inc(wc_done, 1)
                v.wait_ge(wc_done, 2 * b + 2)
                for j in range(NT):
                    n = b * NT + j
                    r = tile_rows(j)
                    lo, hi = j * P, j * P + r
                    o, wj = beats[j % 2], wcol[0:r, j:j + 1]
                    if j >= 2:
                        v.wait_ge(rk_mm, n - 1)
                    wd = wrow[0:r, lo:hi]
                    if j >= 2:
                        v.wait_ge(bt_done, n - 1)
                    v.scalar_tensor_tensor(ties[j % 2][0:r, 0:r], wd, wj, tri[0:r, 0:r], ALU.is_equal, ALU.mult).then_inc(bt_tie, 1)
                    if j > 0:
                        v.tensor_scalar(o[0:r, 0:lo], wrow[0:r, 0:lo], wj, None, ALU.is_lt)
                    if j < NT - 1:
                        v.tensor_scalar(o[0:r, hi:S], wrow[0:r, hi:S], wj, None, ALU.is_le)
                    v.wait_ge(bt_tie, n + 1)
                    v.scalar_tensor_tensor(o[0:r, lo:hi], wd, wj, ties[j % 2][0:r, 0:r], ALU.is_lt, ALU.add).then_inc(bt_done, 1)
                v.wait_ge(rk_mm, (b + 1) * NT)
                for c in range(NCT):
                    v.scalar_tensor_tensor(wrow[:, ch(c)], ps[:, c, 0:CT], TOPK - 0.5, wrow[:, ch(c)],
                                           ALU.is_lt, ALU.mult).then_inc(mw, 1)
                for c in range(NCT):
                    for h in range(CH):
                        n = b * NCT * CH + c * CH + h
                        v.wait_ge(dn_mm, n + 1)
                        if c == 0 and h == 0:
                            v.wait_ge(mw, (b + 1) * NCT)
                        y = ybuf[h]
                        v.scalar_tensor_tensor(y[:], ps[:, 4 + (c * CH + h) % 4, 0:CT], b2_s[:, h:h + 1], wrow[:, ch(c)],
                                               ALU.add, ALU.mult).then_inc(ysc, 1)
                        o = t[:, h, ch(c)]
                        v.tensor_tensor(o, o, xn[:, h, ch(c)], ALU.add).then_inc(yxn, 1)
                        v.wait_ge(ysc, n + 1)
                        v.wait_ge(yxn, n + 1)
                        v.tensor_tensor(o, o, y[:], ALU.add).then_inc(fin, 1)

        @block.tensor
        def _(pe):
            pe.wait_ge(w_in, NW_IN)
            pe.wait_ge(ready0, 2)
            pe.wait_ge(wrb_ready, 1)
            with pe.Fori(0, B) as b:
                norm.pe(pe, b, lambda c: pe.wait_ge(t_in[c], 16 * (b + 1)))
                for c in range(NCT):
                    pe.wait_ge(norm.s_xn_done, b * NCT + c + 1)
                    if c >= 2:
                        pe.wait_ge(r_done, b * NCT + c - 1)
                    for k in range(CH):
                        mm = pe.matmul(ps[:, 4 + c % 2, 0:CT], wrb[:, k, :], xn[:, k, ch(c)], start=(k == 0), stop=(k == CH - 1))
                    mm.then_inc(r_mm, 1)
                pe.wait_ge(r_done, (b + 1) * NCT)
                pe.sem_inc(gate, 1)
                for j in range(NT):
                    r = tile_rows(j)
                    mm = pe.transpose(ps[0:r, 7, j:j + 1], wrow[0:1, j * P:j * P + r], ident[0:1, 0:1])
                mm.then_inc(wc_mm, 1)
                for j in range(NT):
                    r = tile_rows(j)
                    pe.wait_ge(bt_done, b * NT + j + 1)
                    for c in range(NCT):
                        mm = pe.matmul(ps[:, c, 0:CT], ones[0:r, :], beats[j % 2][0:r, ch(c)], start=(j == 0), stop=(j == NT - 1))
                    mm.then_inc(rk_mm, 1)
                pe.wait_ge(mw, (b + 1) * NCT)

                def down(c):
                    pe.wait_ge(gelu, b * NCT * HT + (c + 1) * HT)
                    for h in range(CH):
                        n = c * CH + h
                        if n >= 4:
                            pe.wait_ge(ysc, b * NCT * CH + n - 3)
                        for k in range(HT):
                            mm = pe.matmul(ps[:, 4 + n % 4, 0:CT], w2_s[:, k, h * P:(h + 1) * P], hid[c % 2][:, k, :],
                                           start=(k == 0), stop=(k == HT - 1))
                        mm.then_inc(dn_mm, 1)

                for c in range(NCT):
                    for h in range(HT):
                        n = c * HT + h
                        if n >= 4:
                            pe.wait_ge(gelu, b * NCT * HT + n - 3)
                        for k in range(CH):
                            mm = pe.matmul(ps[:, n % 4, 0:CT], w1_s[:, k, h * P:(h + 1) * P], xn[:, k, ch(c)],
                                           start=(k == 0), stop=(k == CH - 1))
                        mm.then_inc(up_mm, 1)
                    if c >= 1:
                        down(c - 1)
                down(NCT - 1)


def conv_arrays(inp):
    g = lambda n: np.asarray(inp[n])
    col = lambda n: g("L0_conv_" + n)[:REL].reshape(REL, 1)
    a = {}
    a["x"] = g("x").reshape(B, C, H * W)
    a["par32"] = np.concatenate([col(n) for n in ("b1", "b2", "bn1_g", "bn1_b", "bn1_m", "bn1_v", "bn2_g", "bn2_b", "bn2_m", "bn2_v", "cb2")]
                                + [g("L0_conv_b3").reshape(REL, SHARE)], axis=1)
    pc = lambda n: g("L0_conv_" + n)[REL:].reshape(2, 1)
    pp = np.concatenate([g("L0_conv_wp"), g("L0_conv_bp").reshape(2, 1), pc("bn1_g"), pc("bn1_b"), pc("bn1_m"), pc("bn1_v")], axis=1)
    a["parp"] = np.ascontiguousarray(np.broadcast_to(pp[:, None, :], (2, H, 7)))
    w3 = g("L0_conv_w3").reshape(REL, SHARE, C).transpose(1, 0, 2)
    w = np.concatenate([g("L0_conv_w1")[None], g("L0_conv_w2")[None], w3], axis=0)
    a["proj_w"] = np.ascontiguousarray(w.reshape(10, REL, 2, 128).transpose(3, 2, 0, 1))
    lin = np.linspace(-1.0, 1.0, W, dtype=np.float32)
    refl = np.pad(np.arange(W), PAD, mode="reflect")
    tap = np.stack([refl[j:j + W] for j in range(K7)])
    pw = np.stack([np.broadcast_to(lin, (K7, W)), lin[tap]]).reshape(1, 2, K7 * W)
    a["posw"] = np.ascontiguousarray(np.broadcast_to(pw, (2 * H, 2, K7 * W)))
    a["posh"] = np.concatenate([lin.reshape(H, 1), lin[tap].T], axis=1)
    a["cw1pT"] = np.ascontiguousarray(g("L0_conv_cw1")[:, REL:].T)
    a["cw1T"] = np.ascontiguousarray(g("L0_conv_cw1")[:, :REL].T)
    a["cw2T"] = np.ascontiguousarray(g("L0_conv_cw2").T)
    a["group_avg"] = np.kron(np.eye(16, dtype=np.float32), np.full((8, 8), 0.125, np.float32))
    a["ident"] = np.eye(128, dtype=np.float32)
    return {k: np.ascontiguousarray(v) for k, v in a.items()}

def token_arrays(inp):
    g = lambda n: np.asarray(inp[n])
    a = {}
    qkv = g("L1_attn_qkv_w").reshape(3, HG, P, 2, P)
    a["wq"] = qkv[0].transpose(3, 2, 0, 1)
    k = qkv[1].reshape(HG, HPG, DH, 2, P)
    k = np.concatenate([k, k[:, :, :DH // 2]], axis=2).reshape(HG, -1, 2, P)
    a["wkv"] = np.concatenate([k, qkv[2]], axis=1).transpose(3, 2, 0, 1)
    bq = g("L1_attn_qkv_b").reshape(3, HG, P)
    k = bq[1].reshape(HG, HPG, DH)
    k = np.concatenate([k, k[:, :, :DH // 2]], axis=2).reshape(HG, -1)
    k = np.concatenate([k, bq[2]], axis=1)[None]
    a["bkv"] = np.broadcast_to(k, (P,) + k.shape[1:])
    a["bq"] = bq[0].T
    a["projw"] = g("L1_attn_proj_w").T.reshape(HG, P, C).transpose(1, 0, 2)
    a["projb"] = g("L1_attn_proj_b").reshape(2, P).T
    sel = np.zeros((3, DH, FT, 4, DH), np.float32)
    i = np.arange(DH)
    for r in range(DH // 2 + 1):
        sel[:, i, r // 4, r % 4, i] = 1
        sel[:, (i + r) % DH, r // 4, r % 4, i] = 1
    for r in (1, 2):
        sel[:, i, FT - 1, r, i] = 1
    a["sel"] = sel.reshape(3 * DH, FT, P)
    selb = np.zeros((P, 1), np.float32)
    selb[DH:2 * DH], selb[2 * DH:3 * DH], selb[3 * DH] = 1, -1, 1
    a["selb"] = selb
    a["heads"] = np.kron(np.eye(HPG, dtype=np.float32), np.ones((DH, DH), np.float32))
    a["avg"] = np.full((P, P), 1.0 / C, np.float32)
    a["wr"] = g("L1_ffn_wr").reshape(2, P).T
    a["br"] = np.broadcast_to(g("L1_ffn_br").reshape(1, 1), (P, 1))
    a["w1"] = g("L1_ffn_w1").reshape(2, P, 4 * C).transpose(1, 0, 2)
    a["b1"] = g("L1_ffn_b1").reshape(8, P).T
    a["w2"] = g("L1_ffn_w2").reshape(8, P, C).transpose(1, 0, 2)
    a["b2"] = g("L1_ffn_b2").reshape(2, P).T
    a["tri"] = np.triu(np.ones((P, P), np.float32), 1)
    return {k: np.ascontiguousarray(v) for k, v in a.items()}


def hybrid_kernel(nc, d, out):
    ctx = ExitStack()
    with ctx:
        planes = nc.dram_tensor("planes", (P, HP, SHARE, WP), F32, kind="Internal").ap()
        x2_dram = nc.dram_tensor("x2_dram", (P, HP, WP), F32, kind="Internal").ap()
        x1_dram = nc.dram_tensor("x1_dram", (P, S), F32, kind="Internal").ap()
        pf_dram = nc.dram_tensor("pf_dram", (6, K7, H, K7 * W), BF16, kind="Internal").ap()
        conv_dram = nc.dram_tensor("conv_dram", (B, C, S), F32, kind="Internal").ap()
        t2_dram = nc.dram_tensor("t2_dram", (B, C, S), F32, kind="Internal").ap()
        keep = {"ps": ctx.enter_context(nc.psum_tensor("ps", [P, 8, 512], F32)),
                "par": ctx.enter_context(nc.sbuf_tensor("par", [P, NPAR], F32)),
                "cw1p18": ctx.enter_context(nc.sbuf_tensor("cw1p18", [18, P], BF16))}
        for n in ("s1c", "t1c", "t2c", "s2c", "u2c"):
            keep[n] = ctx.enter_context(nc.sbuf_tensor(n, [P, 1], F32))
        project_stage(nc, d["x"], d["par32"], d["parp"], d["proj_w"], d["posw"], d["posh"], d["cw1pT"],
                      d["group_avg"], planes, x2_dram, x1_dram, pf_dram, keep)
        conv_stage(nc, planes, x2_dram, x1_dram, pf_dram, d["cw1T"], d["cw2T"], d["ident"], conv_dram, keep)
        attention_stage(nc, d["x"], conv_dram, t2_dram, d["wq"], d["wkv"], d["bkv"], d["bq"], d["projw"], d["projb"],
                        d["sel"], d["selb"], d["heads"], d["avg"], d["ident"], keep)
        routed_stage(nc, t2_dram, out, d["wr"], d["br"], d["w1"], d["b1"], d["w2"], d["b2"], d["avg"], d["ident"],
                     d["tri"], keep)


def kernel(**inputs):
    import concourse.bacc as bacc
    from concourse.bass_utils import run_bass_kernel_spmd

    nc = bacc.Bacc("TRN2", target_bir_lowering=False, num_devices=1)
    arrays = {"in_" + k: v for k, v in (conv_arrays(inputs) | token_arrays(inputs)).items()}
    d = {k[3:]: nc.dram_tensor(k, v.shape, mybir.dt.from_np(v.dtype), kind="ExternalInput").ap() for k, v in arrays.items()}
    out = nc.dram_tensor("out_dram", (B, C, S), F32, kind="ExternalOutput").ap()
    hybrid_kernel(nc, d, out)
    r = run_bass_kernel_spmd(nc, [arrays], core_ids=[0])
    return r.results[0]["out_dram"].reshape(B, C, H, W)
```

```python
import numpy as np
import concourse.bass as bass
from concourse import mybir
from contextlib import ExitStack

F32 = mybir.dt.float32
BF16 = mybir.dt.bfloat16
ALU = mybir.AluOpType
ACT = mybir.ActivationFunctionType
AX = mybir.AxisListType

B, C, H, W = 4, 256, 56, 56
S = H * W
P = 128
CH = C // P
K7, PAD = 7, 3
REL = 32
SHARE = C // REL
WP = W + 2 * PAD
HP = H + 2 * PAD
NOUT = SHARE + 2
PL = SHARE + 1
RB = 8
NBK = H // RB
CB = RB * W
RW = 4
NW = H // RW
PW = RW * W
TAPS = K7 * K7
GN_EPS, BN_EPS = 1e-5, 1e-5

B1, B2, G1, BE1, M1, V1, G2, BE2, M2, V2, CB2, B3 = range(12)
NPAR = B3 + SHARE
WPX, WPY, BP, GP, BEP, MP, VP = range(7)


def project_stage(nc, x, par32, parp, proj_w, posw, posh, cw1pT, group_avg, planes, x2_dram, a1_dram, pf_dram, keep):
    ctx = ExitStack()
    with ctx:
        def sb(name, shape, dt=F32):
            return ctx.enter_context(nc.sbuf_tensor(name, shape, dt))

        def sem(name):
            return ctx.enter_context(nc.semaphore(name))

        xs = sb("xs", [P, B, CH, S])
        wts = sb("wts", [P, CH, NOUT, REL])
        gav = sb("gav", [P, P])
        stats = sb("stats", [P, B * CH, NBK, 6])
        mv = sb("mv", [P, B * CH, 2])
        mom = sb("mom", [P, 2, B * CH])
        gmom = sb("gmom", [P, 2, B * CH])
        gvar = sb("gvar", [P, B * CH])
        gstd = sb("gstd", [P, B * CH])
        grs = sb("grs", [P, B * CH])
        gnb = sb("gnb", [P, B * CH])
        stage = sb("stage", [P, 2, RB, PL, WP])
        a1s = sb("a1s", [P, 2, CB])
        fold = sb("fold", [P, 8])
        pwt = sb("pwt", [2 * H, 2, K7 * W])
        pht = sb("pht", [2 * H, 1 + K7])
        ppt = sb("ppt", [2 * H, 7])
        pq = sb("pq", [2 * H, 2, K7 * W])
        ud = sb("ud", [2 * H, K7 * W])
        hq = sb("hq", [2 * H, 1 + K7])
        vd = sb("vd", [2 * H, K7])
        pfold = sb("pfold", [2 * H, 3])
        feat = sb("feat", [2 * H, K7, K7 * W])
        fparts = sb("fparts", [2 * H, 3, K7, K7 * W], BF16)
        cwp = sb("cwp", [2, P])
        cwparts = sb("cwparts", [2, 3, P], BF16)
        ps = keep["ps"]

        par, cw1p18, s1c, t1c, t2c, s2c, u2c = (keep[k] for k in ("par", "cw1p18", "s1c", "t1c", "t2c", "s2c", "u2c"))

        x_in = [sem(f"x_in{n}") for n in range(B * CH)]
        small_in = sem("small_in")
        stat_done = sem("stat_done")
        mom_done = sem("mom_done")
        gmom_mm = sem("gmom_mm")
        gstep = sem("gstep")
        gsqrt = sem("gsqrt")
        fstep = sem("fstep")
        fsqrt = sem("fsqrt")
        normed = sem("normed")
        pstep = sem("pstep")
        feat_done = sem("feat_done")
        parts = sem("parts")
        proj_done = sem("proj_done")
        evac_a = sem("evac_a")
        evac_v = sem("evac_v")
        padded = sem("padded")
        stored = [sem(f"stored{k}") for k in range(2)]
        pf_out = sem("pf_out")
        cwp_out = sem("cwp_out")

        x_v = x.rearrange("b (k p) s -> b k p s", p=P)
        NPARTS = 6
        N_SMALL = 16 * (1 + 1 + 4 + 4 + 1 + 2 + 2)
        DVE_OUT = (3, 5, 7, 9)
        ACT_OUT = tuple(o for o in range(NOUT) if o not in DVE_OUT)
        block = ctx.enter_context(nc.Block())

        @block.sync
        def _(sp):
            def position_features():
                sp.wait_ge(parts, NPARTS)
                for f in range(3):
                    for c in range(2):
                        sp.dma_start(pf_dram[2 * f + c].rearrange("i h x -> h i x"),
                                     fparts[c * H:(c + 1) * H, f]).then_inc(pf_out, 16)
                for w in range(3):
                    for f in range(3):
                        sp.dma_start(cw1p18[w * 6 + f * 2:w * 6 + f * 2 + 2, :], cwparts[:, w, :]).then_inc(cwp_out, 16)

            for b in range(B):
                for k in range(CH):
                    sp.dma_start(xs[:, b, k, :], x_v[b, k]).then_inc(x_in[b * CH + k], 16)
            for blk in range(NBK):
                s = blk % 2
                sp.wait_ge(evac_a, len(ACT_OUT) * (blk + 1))
                sp.wait_ge(evac_v, len(DVE_OUT) * (blk + 1))
                sp.wait_ge(padded, 2 * (blk + 1))
                r0 = PAD + blk * RB
                sp.dma_start(planes[:, r0:r0 + RB], stage[:, s, :, 0:SHARE]).then_inc(stored[s], 16)
                sp.dma_start(x2_dram[:, r0:r0 + RB], stage[:, s, :, SHARE]).then_inc(stored[s], 16)
                sp.dma_start(a1_dram[:, blk * CB:(blk + 1) * CB], a1s[:, s]).then_inc(stored[s], 16)
                if blk == 0:
                    for r in range(PAD):
                        sp.dma_start(planes[:, r], stage[:, s, PAD - r, 0:SHARE]).then_inc(stored[s], 16)
                        sp.dma_start(x2_dram[:, r], stage[:, s, PAD - r, SHARE]).then_inc(stored[s], 16)
                if blk == 1:
                    position_features()
                if blk == NBK - 1:
                    for r in range(PAD):
                        sp.dma_start(planes[:, PAD + H + r], stage[:, s, RB - 2 - r, 0:SHARE]).then_inc(stored[s], 16)
                        sp.dma_start(x2_dram[:, PAD + H + r], stage[:, s, RB - 2 - r, SHARE]).then_inc(stored[s], 16)
            sp.wait_ge(stored[0], 16 * (3 * ((NBK + 1) // 2) + 4 * PAD))
            sp.wait_ge(stored[1], 16 * (3 * (NBK // 2)))
            sp.wait_ge(pf_out, 16 * 6)
            sp.wait_ge(cwp_out, 16 * 9)

        @block.gpsimd
        def _(pool):
            pool.dma_start(wts[:], proj_w).then_inc(small_in, 16)
            pool.dma_start(gav[:], group_avg).then_inc(small_in, 16)
            for q in range(4):
                pool.dma_start(par[32 * q:32 * q + 32, :], par32).then_inc(small_in, 16)
                pool.dma_start(cwp[:, 32 * q:32 * q + 32], cw1pT).then_inc(small_in, 16)
            pool.dma_start(pwt[:], posw).then_inc(small_in, 16)
            for c in range(2):
                pool.dma_start(pht[c * H:(c + 1) * H, :], posh).then_inc(small_in, 16)
                pool.dma_start(ppt[c * H:(c + 1) * H, :], parp[c]).then_inc(small_in, 16)
            for blk in range(NBK):
                s = blk % 2
                pool.wait_ge(evac_a, len(ACT_OUT) * (blk + 1))
                pool.wait_ge(evac_v, len(DVE_OUT) * (blk + 1))
                for k in range(PAD):
                    for dst, src in ((PAD - 1 - k, PAD + 1 + k), (PAD + W + k, PAD + W - 2 - k)):
                        last = pool.tensor_copy(stage[:, s, :, :, dst:dst + 1], stage[:, s, :, :, src:src + 1])
                        if k == PAD - 1:
                            last.then_inc(padded, 1)

        @block.scalar
        def _(act):
            act.wait_ge(fstep, 2)
            act.activation(fold[:, 2:4], fold[:, 0:2], ACT.Sqrt).then_inc(fsqrt, 1)
            act.wait_ge(pstep, 2)
            act.activation(pfold[:, 1:2], pfold[:, 0:1], ACT.Sqrt).then_inc(fsqrt, 1)
            act.wait_ge(gstep, 4)
            act.activation(gstd[:], gvar[:], ACT.Sqrt).then_inc(gsqrt, 1)
            act.wait_ge(pstep, 10)
            for i in range(K7):
                act.activation(feat[:, i, :], ud[:], ACT.Relu, scale=pfold[:, 2:3],
                               bias=vd[:, i:i + 1]).then_inc(feat_done, 1)
            for blk in range(NBK):
                s = blk % 2
                if blk >= 2:
                    act.wait_ge(stored[s], 16 * (3 * (blk // 2) + (2 * PAD if s == 0 else 0)))
                for o in ACT_OUT:
                    act.wait_ge(proj_done, blk * NOUT + o + 1)
                    src = ps[:, (blk * NOUT + o) % 8, 0:CB]
                    if o == 0:
                        act.activation(a1s[:, s, :], src, ACT.Identity, scale=s1c[:], bias=t1c[:]).then_inc(evac_a, 1)
                    elif o == 1:
                        act.activation(stage[:, s, :, SHARE, PAD:PAD + W], src.rearrange("p (h w) -> p h w", w=W),
                                       ACT.Identity, scale=s1c[:], bias=t2c[:]).then_inc(evac_a, 1)
                    else:
                        act.activation(stage[:, s, :, o - 2, PAD:PAD + W], src.rearrange("p (h w) -> p h w", w=W),
                                       ACT.Identity, bias=par[:, B3 + o - 2:B3 + o - 1]).then_inc(evac_a, 1)

        @block.vector
        def _(v):
            for n in range(B * CH):
                v.wait_ge(x_in[n], 16)
                for q in range(NBK):
                    v.bn_stats(stats[:, n, q, :], xs[:, n // CH, n % CH, q * CB:(q + 1) * CB]).then_inc(stat_done, 1)
                v.wait_ge(stat_done, NBK * (n + 1))
                v.bn_aggr(mv[:, n, :], stats[:, n]).then_inc(mom_done, 1)
            v.wait_ge(mom_done, B * CH)
            v.tensor_copy(mom[:, 0, :], mv[:, :, 0]).then_inc(gstep, 1)
            v.tensor_tensor(mom[:, 1, :], mv[:, :, 0], mv[:, :, 0], ALU.mult).then_inc(gstep, 1)
            v.wait_ge(gstep, 2)
            v.tensor_tensor(mom[:, 1, :], mom[:, 1, :], mv[:, :, 1], ALU.add).then_inc(mom_done, 1)
            v.wait_ge(small_in, N_SMALL)
            v.tensor_scalar(fold[:, 0:1], par[:, V1:V1 + 1], BN_EPS, None, ALU.add).then_inc(fstep, 1)
            v.tensor_scalar(fold[:, 1:2], par[:, V2:V2 + 1], BN_EPS, None, ALU.add).then_inc(fstep, 1)
            v.tensor_scalar(pq[:], pwt[:], ppt[:, WPX:WPX + 1], ppt[:, BP:BP + 1], ALU.mult, ALU.add).then_inc(pstep, 1)
            v.tensor_scalar(pfold[:, 0:1], ppt[:, VP:VP + 1], BN_EPS, None, ALU.add).then_inc(pstep, 1)
            v.tensor_scalar(hq[:], pht[:], ppt[:, WPY:WPY + 1], None, ALU.mult).then_inc(pstep, 1)
            v.wait_ge(pstep, 3)
            v.tensor_tensor(ud[:], pq[:, 0, :], pq[:, 1, :], ALU.subtract).then_inc(pstep, 1)
            v.tensor_scalar(vd[:], hq[:, 1:1 + K7], hq[:, 0:1], -1.0, ALU.subtract, ALU.mult).then_inc(pstep, 1)
            v.wait_ge(fsqrt, 2)
            v.reciprocal(fold[:, 4:6], fold[:, 2:4]).then_inc(fstep, 1)
            v.reciprocal(pfold[:, 2:3], pfold[:, 1:2]).then_inc(pstep, 1)
            v.wait_ge(fstep, 3)
            v.wait_ge(pstep, 6)
            v.tensor_tensor(s1c[:], par[:, G1:G1 + 1], fold[:, 4:5], ALU.mult).then_inc(fstep, 1)
            v.tensor_tensor(s2c[:], par[:, G2:G2 + 1], fold[:, 5:6], ALU.mult).then_inc(fstep, 1)
            v.tensor_tensor(pfold[:, 2:3], ppt[:, GP:GP + 1], pfold[:, 2:3], ALU.mult).then_inc(pstep, 1)
            v.wait_ge(fstep, 5)
            v.wait_ge(pstep, 7)
            v.tensor_scalar(fold[:, 6:7], par[:, B1:B1 + 1], par[:, M1:M1 + 1], s1c[:], ALU.subtract, ALU.mult).then_inc(fstep, 1)
            v.tensor_tensor(t2c[:], par[:, B2:B2 + 1], s1c[:], ALU.mult).then_inc(fstep, 1)
            v.tensor_tensor(fold[:, 7:8], par[:, M2:M2 + 1], s2c[:], ALU.mult).then_inc(fstep, 1)
            v.tensor_scalar(vd[:], vd[:], ppt[:, MP:MP + 1], pfold[:, 2:3], ALU.subtract, ALU.mult).then_inc(pstep, 1)
            v.wait_ge(fstep, 8)
            v.wait_ge(pstep, 8)
            v.tensor_tensor(t1c[:], fold[:, 6:7], par[:, BE1:BE1 + 1], ALU.add).then_inc(fstep, 1)
            v.tensor_tensor(u2c[:], par[:, BE2:BE2 + 1], fold[:, 7:8], ALU.subtract).then_inc(fstep, 1)
            v.tensor_scalar(vd[:], vd[:], ppt[:, BEP:BEP + 1], None, ALU.add).then_inc(pstep, 1)
            v.tensor_copy(cwparts[:, 0, :], cwp[:]).then_inc(parts, 1)
            v.wait_ge(parts, 1)
            v.tensor_tensor(cwp[:], cwp[:], cwparts[:, 0, :], ALU.subtract).then_inc(pstep, 1)
            v.wait_ge(pstep, 10)
            v.tensor_copy(cwparts[:, 1, :], cwp[:]).then_inc(parts, 1)
            v.wait_ge(parts, 2)
            v.tensor_tensor(cwparts[:, 2, :], cwp[:], cwparts[:, 1, :], ALU.subtract).then_inc(parts, 1)

            v.wait_ge(gmom_mm, 1)
            v.tensor_copy(gmom[:], ps[:, 0, 0:2 * B * CH].rearrange("p (a n) -> p a n", a=2)).then_inc(mom_done, 1)
            v.wait_ge(mom_done, B * CH + 2)
            v.tensor_tensor(gvar[:], gmom[:, 0, :], gmom[:, 0, :], ALU.mult).then_inc(gstep, 1)
            v.wait_ge(gstep, 3)
            v.scalar_tensor_tensor(gvar[:], gmom[:, 1, :], GN_EPS, gvar[:], ALU.add, ALU.subtract).then_inc(gstep, 1)
            v.wait_ge(gsqrt, 1)
            v.reciprocal(grs[:], gstd[:]).then_inc(gstep, 1)
            v.wait_ge(gstep, 5)
            v.scalar_tensor_tensor(gnb[:], gmom[:, 0, :], -1.0, grs[:], ALU.mult, ALU.mult).then_inc(gstep, 1)
            v.wait_ge(gstep, 6)
            def normalize(blk):
                for n in range(B * CH):
                    xv = xs[:, n // CH, n % CH, blk * CB:(blk + 1) * CB]
                    v.tensor_scalar(xv, xv, grs[:, n:n + 1], gnb[:, n:n + 1], ALU.mult, ALU.add).then_inc(normed, 1)

            normalize(0)
            normalize(1)
            for blk in range(NBK):
                s = blk % 2
                if blk >= 2:
                    v.wait_ge(stored[s], 16 * (3 * (blk // 2) + (2 * PAD if s == 0 else 0)))
                for o in DVE_OUT:
                    v.wait_ge(proj_done, blk * NOUT + o + 1)
                    v.tensor_scalar(stage[:, s, :, o - 2, PAD:PAD + W],
                                    ps[:, (blk * NOUT + o) % 8, 0:CB].rearrange("p (h w) -> p h w", w=W),
                                    par[:, B3 + o - 2:B3 + o - 1], None, ALU.add).then_inc(evac_v, 1)
                if blk + 2 < NBK:
                    normalize(blk + 2)
                if blk != 1:
                    continue
                v.wait_ge(feat_done, K7)
                v.tensor_copy(fparts[:, 0], feat[:]).then_inc(parts, 1)
                v.wait_ge(parts, 4)
                v.tensor_tensor(feat[:], feat[:], fparts[:, 0], ALU.subtract).then_inc(pstep, 1)
                v.wait_ge(pstep, 11)
                v.tensor_copy(fparts[:, 1], feat[:]).then_inc(parts, 1)
                v.wait_ge(parts, 5)
                v.tensor_tensor(fparts[:, 2], feat[:], fparts[:, 1], ALU.subtract).then_inc(parts, 1)

        @block.tensor
        def _(pe):
            pe.wait_ge(small_in, N_SMALL)
            pe.wait_ge(mom_done, B * CH + 1)
            pe.matmul(ps[:, 0, 0:2 * B * CH], gav[:], mom[:].rearrange("p a n -> p (a n)"),
                      start=True, stop=True).then_inc(gmom_mm, 1)
            pe.wait_ge(mom_done, B * CH + 2)
            for blk in range(NBK):
                pe.wait_ge(normed, B * CH * (blk + 1))
                for o in range(NOUT):
                    n = blk * NOUT + o
                    if n >= 8:
                        m = n - 8
                        mb, mo = m // NOUT, m % NOUT
                        if mo in DVE_OUT:
                            pe.wait_ge(evac_v, mb * len(DVE_OUT) + DVE_OUT.index(mo) + 1)
                        else:
                            pe.wait_ge(evac_a, mb * len(ACT_OUT) + ACT_OUT.index(mo) + 1)
                    for k in range(CH):
                        for b in range(B):
                            mm = pe.matmul(ps[32 * b:32 * b + 32, n % 8, 0:CB], wts[:, k, o, :],
                                           xs[:, b, k, blk * CB:(blk + 1) * CB], start=(k == 0), stop=(k == CH - 1))
                    mm.then_inc(proj_done, 1)


PAIRS = 10
PAIRS_BY = 30


def tap_units():
    units, t, made = [], 0, 0
    while t < TAPS:
        want = min(PAIRS, (len(units) + 1) * PAIRS // PAIRS_BY)
        if made < want and t % K7 < K7 - 1:
            units.append((t, t + 1))
            t, made = t + 2, made + 1
        else:
            units.append((t,))
            t += 1
    return units


UNITS = tap_units()
NU = len(UNITS)
NPAIR = sum(len(u) == 2 for u in UNITS)
NPROD = 3
assert NU % NPROD == 0
Z_AT = [max(0, RW * i - 2) for i in range(K7)]
ROW_MAX_AT = [7 + 4 * i for i in range(K7)]
SHIFT_AT = [31, 32, 33, 34, 35, 36, 37]
ROW_SUM_AT = [6 + 3 * i for i in range(K7)]
DEN_AT = 28
CPI = RW
NCH = K7 * CPI
CW = K7 * W


class Blk:

    def __init__(self, it, c):
        self.it, self.c = it, c
        self.n = 2 * it + c
        self.par = c % 2
        self.half = it + c // 2

    def q(self, i):
        return self.n * K7 + i

    def qpar(self, i):
        return (self.c * K7 + i) % 2

    def qhalf(self, i):
        return self.it * K7 + (self.c * K7 + i) // 2 + 1

    def g(self, c):
        return self.n * NCH + c

    def early(self, m):
        return isinstance(self.n, int) and self.n < m


def conv_stage(nc, planes, x2_dram, a1_dram, pf_dram, cw1_bd, cw2_bd, ident_dram, conv_dram, keep):
    ctx = ExitStack()
    with ctx:
        def sb(name, shape, dt=F32):
            return ctx.enter_context(nc.sbuf_tensor(name, shape, dt))

        def sem(name):
            return ctx.enter_context(nc.semaphore(name))

        win = [sb(f"win{k}", [P, RW + K7 - 1, SHARE, WP]) for k in range(2)]
        x2w = [sb(f"x2w{k}", [P, RW + K7 - 1, WP]) for k in range(2)]
        a1 = [sb(f"a1w{k}", [P, PW]) for k in range(2)]
        lg = [sb(f"lg{k}", [P, K7, K7, PW]) for k in range(2)]
        y1 = [sb(f"y1{k}", [P, K7, PW]) for k in range(2)]
        y2 = [sb(f"y2{k}", [P, CW]) for k in range(2)]
        prod = [sb(f"prod{k}", [P, SHARE, PW]) for k in range(NPROD)]
        prodb = sb("prodb", [P, SHARE, PW])
        pf = [sb(f"pf{k}", [18, RW, CW], BF16) for k in range(2)]
        osb = sb("osb", [P, SHARE, PW])
        mx = sb("mx", [P, PW])
        rmax = sb("rmax", [P, K7, PW])
        rsum = sb("rsum", [P, K7, PW])
        den = [sb(f"den{k}", [P, PW]) for k in range(2)]
        cw1 = sb("cw1bd", [P, P])
        cw2 = sb("cw2bd", [P, P])
        ident = sb("ident1", [P, P])
        ps = keep["ps"]
        y2p, lgp, acc = ps[:, 0:2], ps[:, 2:4], ps[:, 4:8]
        par, cw1p18, s2c, u2c = (keep[k] for k in ("par", "cw1p18", "s2c", "u2c"))

        w_in = sem("w_in")
        win_in = [sem(f"win_in{k}") for k in range(2)]
        x_in = [sem(f"x12_in{k}") for k in range(2)]
        pf_in = [sem(f"pf_in{k}") for k in range(2)]
        z_ready = sem("z_ready")
        relu1 = sem("relu1")
        mm1 = sem("mm1")
        relu2 = sem("relu2")
        mm2 = sem("mm2")
        logit = sem("logit")
        maxed = sem("maxed")
        rowmax = sem("rowmax")
        rowsum = sem("rowsum")
        shifted = sem("shifted")
        exped = sem("exped")
        densum = sem("densum")
        rden = sem("rden")
        pairmul = sem("pairmul")
        prod_ready = sem("prod_ready")
        summed = sem("summed")
        outn = sem("outn")
        stored = sem("stored1")

        conv_v = conv_dram.rearrange("b (l s) x -> (b l) s x", s=SHARE)
        block = ctx.enter_context(nc.Block())

        def slots(eng, slot):
            slot(Blk(0, 0), None)
            slot(Blk(0, 1), Blk(0, 0))
            with eng.Fori(0, NW // 2 - 1) as it:
                slot(Blk(it, 2), Blk(it, 1))
                slot(Blk(it, 3), Blk(it, 2))
            slot(None, Blk(0, NW - 1))

        @block.gpsimd
        def _(pool):
            def load(a):
                if not a.early(2):
                    pool.wait_ge(z_ready, a.q(0) - K7)
                pool.dma_start(x2w[a.par][:], x2_dram[:, bass.ds(a.n * RW, RW + K7 - 1)]).then_inc(x_in[a.par], 16)
                pool.dma_start(a1[a.par][:], a1_dram[:, bass.ds(a.n * PW, PW)]).then_inc(x_in[a.par], 16)
                if not a.early(2):
                    pool.wait_ge(prod_ready, NU * (a.n - 1))
                pool.dma_start(win[a.par][:], planes[:, bass.ds(a.n * RW, RW + K7 - 1)]).then_inc(win_in[a.par], 16)

            slots(pool, lambda a, b: a and load(a))

        @block.sync
        def _(sp):
            def store(n):
                if isinstance(n, int) and n < 0:
                    return
                sp.wait_ge(outn, n + 1)
                sp.dma_start(conv_v[:, :, bass.ds(n * PW, PW)], osb[:]).then_inc(stored, 16)

            def slot(a, b):
                if a:
                    for i in range(K7):
                        k = a.qpar(i)
                        if not (a.early(1) and i < 2):
                            sp.wait_ge(mm1, CPI * (a.q(i) - 1))
                        for w in range(3):
                            sp.dma_start(pf[k][6 * w:6 * w + 6], pf_dram[:, i, bass.ds(a.n * RW, RW)]).then_inc(pf_in[k], 16)
                        if b and i == 1:
                            store(b.n - 1)
                elif b:
                    store(b.n - 1)
                if b and not a:
                    store(b.n)

            slots(sp, slot)
            sp.wait_ge(stored, 16 * NW)

        @block.scalar
        def _(act):
            def slot(a, b):
                if not a:
                    return

                def first(i):
                    act.wait_ge(z_ready, a.q(i) + 1)
                    t = y1[a.qpar(i)]
                    act.activation(t[:], t[:], ACT.Relu).then_inc(relu1, 1)

                def second(c):
                    g = a.g(c)
                    act.wait_ge(mm1, g + 1)
                    if not (a.early(1) and c < 2):
                        act.wait_ge(mm2, g - 1)
                    act.activation(y2[c % 2][:], y2p[:, c % 2, 0:CW], ACT.Relu, scale=s2c[:],
                                   bias=u2c[:]).then_inc(relu2, 1)

                def third(c):
                    act.wait_ge(mm2, a.g(c) + 1)
                    if c == 0 and not a.early(2):
                        act.wait_ge(prod_ready, NU * (a.n - 1))
                        act.wait_ge(rowsum, a.q(0) - K7)
                    i, h = c // CPI, c % CPI
                    act.activation(lg[a.par][:, i, :, h * W:(h + 1) * W],
                                   lgp[:, c % 2, 0:CW].rearrange("p (j w) -> p j w", w=W),
                                   ACT.Identity, bias=par[:, CB2:CB2 + 1]).then_inc(logit, 1)

                first(0)
                for c in range(NCH):
                    second(c)
                    if c >= 1:
                        third(c - 1)
                    if c % CPI == CPI - 2 and c // CPI + 1 < K7:
                        first(c // CPI + 1)
                third(NCH - 1)
                for i in range(K7):
                    act.wait_ge(shifted, a.q(i) + 1)
                    act.activation(lg[a.par][:, i], lg[a.par][:, i], ACT.Exp).then_inc(exped, 1)

            act.dma_start(cw1[:], cw1_bd).then_inc(w_in, 16)
            act.dma_start(cw2[:], cw2_bd).then_inc(w_in, 16)
            act.dma_start(ident[:], ident_dram).then_inc(w_in, 16)
            slots(act, slot)

        @block.vector
        def _(v):
            def slot(a, b):
                def z(i):
                    q = a.q(i)
                    if i == 0:
                        v.wait_ge(x_in[a.par], 32 * (a.half + 1))
                    if not (a.early(1) and i < 2):
                        v.wait_ge(mm1, CPI * (q - 1))
                    o = y1[a.qpar(i)][:].rearrange("p j (h w) -> p j h w", w=W)
                    x1 = a1[a.par][:].rearrange("p (h w) -> p h w", w=W).unsqueeze(1).broadcast_to([P, K7, RW, W])
                    row = x2w[a.par][:, i:i + RW, 0:W]
                    x2 = bass.AP(row.tensor, row.offset, [row.ap[0], [1, K7], row.ap[1], row.ap[2]])
                    v.tensor_tensor(o, x1, x2, ALU.subtract).then_inc(z_ready, 1)

                def row_max(i):
                    v.wait_ge(logit, a.g(0) + CPI * (i + 1))
                    v.tensor_reduce(rmax[:, i], lg[a.par][:, i].rearrange("p j x -> p x j"), AX.X, ALU.max).then_inc(rowmax, 1)

                def all_max():
                    v.wait_ge(rowmax, a.q(K7))
                    v.tensor_reduce(mx[:], rmax[:].rearrange("p i x -> p x i"), AX.X, ALU.max).then_inc(maxed, 1)

                def shift(i):
                    v.wait_ge(maxed, a.n + 1)
                    l = lg[a.par][:, i]
                    v.tensor_tensor(l, l, mx[:].unsqueeze(1).broadcast_to([P, K7, PW]), ALU.subtract).then_inc(shifted, 1)

                def row_sum(i):
                    v.wait_ge(exped, b.q(i) + 1)
                    v.tensor_reduce(rsum[:, i], lg[b.par][:, i].rearrange("p j x -> p x j"), AX.X, ALU.add).then_inc(rowsum, 1)

                def denominators():
                    v.wait_ge(rowsum, b.q(K7))
                    v.tensor_reduce(den[b.par][:], rsum[:].rearrange("p i x -> p x i"), AX.X, ALU.add).then_inc(densum, 1)
                    v.wait_ge(densum, b.n + 1)
                    v.reciprocal(den[b.par][:], den[b.par][:]).then_inc(rden, 1)

                def mult(t, out):
                    i, j = t // K7, t % K7
                    w = lg[b.par][:, i, j].rearrange("p (h w) -> p h w", w=W).unsqueeze(1).broadcast_to([P, SHARE, RW, W])
                    xw = win[b.par][:, i:i + RW, 0:SHARE, j:j + W].rearrange("p h s w -> p s h w")
                    return v.tensor_tensor(out[:].rearrange("p s (h w) -> p s h w", w=W), w, xw, ALU.mult)

                def unit(u):
                    taps = UNITS[u]
                    if u == 0:
                        v.wait_ge(win_in[b.par], 16 * (b.half + 1))
                    v.wait_ge(exped, b.q(taps[-1] // K7) + 1)
                    if not (b.early(1) and u < NPROD):
                        v.wait_ge(summed, NU * b.n + u + 1 - NPROD)
                    out = prod[u % NPROD]
                    if len(taps) == 1:
                        mult(taps[0], out).then_inc(prod_ready, 1)
                    else:
                        k = sum(len(x) == 2 for x in UNITS[:u])
                        mult(taps[0], out).then_inc(pairmul, 1)
                        last = max([y for y in range(u) if len(UNITS[y]) == 2], default=-NPROD)
                        if u - last < NPROD:
                            v.wait_ge(prod_ready, NU * b.n + last + 1)
                        mult(taps[1], prodb).then_inc(pairmul, 1)
                        v.wait_ge(pairmul, 2 * (NPAIR * b.n + k + 1))
                        v.tensor_tensor(out[:], out[:], prodb[:], ALU.add).then_inc(prod_ready, 1)

                def normalize(d, n):
                    v.wait_ge(summed, NU * (n + 1))
                    v.wait_ge(rden, n + 1)
                    if not (isinstance(n, int) and n == 0):
                        v.wait_ge(stored, 16 * n)
                    v.tensor_tensor(osb[:].rearrange("p (q t) x -> p q t x", t=2),
                                    acc[:, :, 0:2 * PW].rearrange("p q (t x) -> p q t x", t=2),
                                    d[:].unsqueeze(1).unsqueeze(1).broadcast_to([P, 4, 2, PW]),
                                    ALU.mult).then_inc(outn, 1)

                if not b:
                    for i in range(K7 + 2):
                        if i < K7:
                            z(i)
                        if i >= 2:
                            row_max(i - 2)
                    all_max()
                    for i in range(K7):
                        shift(i)
                    return
                for u in range(NU):
                    for i in range(K7):
                        if a and u == Z_AT[i]:
                            z(i)
                    if a and u in ROW_MAX_AT:
                        row_max(ROW_MAX_AT.index(u))
                    if u == 1 and not b.early(1):
                        normalize(den[1 - b.par], b.n - 1)
                    if u in ROW_SUM_AT:
                        row_sum(ROW_SUM_AT.index(u))
                    if u == DEN_AT:
                        denominators()
                    if a and u == SHIFT_AT[0]:
                        all_max()
                    for i in range(K7):
                        if a and u == SHIFT_AT[i]:
                            shift(i)
                    unit(u)
                if not a:
                    normalize(den[b.par], b.n)

            slots(v, slot)

        @block.tensor
        def _(pe):
            def slot(a, b):
                def first(c):
                    i, h = c // CPI, c % CPI
                    g = a.g(c)
                    if h == 0:
                        pe.wait_ge(relu1, a.q(i) + 1)
                        pe.wait_ge(pf_in[a.qpar(i)], 48 * a.qhalf(i))
                    if not (a.early(1) and c < 2):
                        pe.wait_ge(relu2, g - 1)
                    out = y2p[:, c % 2, 0:CW]
                    pe.matmul(out.rearrange("p (j w) -> p j w", w=W), cw1[:], y1[a.qpar(i)][:, :, h * W:(h + 1) * W], start=True, stop=False)
                    pe.matmul(out, cw1p18[:], pf[a.qpar(i)][:, h, :], start=False, stop=True).then_inc(mm1, 1)

                def second(c):
                    g = a.g(c)
                    pe.wait_ge(relu2, g + 1)
                    if not (a.early(1) and c < 2):
                        pe.wait_ge(logit, g - 1)
                    pe.matmul(lgp[:, c % 2, 0:CW], cw2[:], y2[c % 2][:], start=True, stop=True).then_inc(mm2, 1)

                def unit(u):
                    pe.wait_ge(prod_ready, NU * b.n + u + 1)
                    if u == 0 and not b.early(1):
                        pe.wait_ge(outn, b.n)
                    for q in range(4):
                        mm = pe.matmul(acc[:, q, 0:2 * PW], ident[:], prod[u % NPROD][:, 2 * q:2 * q + 2, :].rearrange("p s x -> p (s x)"),
                                       start=(u == 0), stop=(u == NU - 1))
                    mm.then_inc(summed, 1)

                if not b:
                    for c in range(NCH + 1):
                        if c < NCH:
                            first(c)
                        if c >= 1:
                            second(c - 1)
                    return
                for u in range(NU):
                    if a and u < NCH:
                        first(u)
                    if a and 1 <= u < 1 + NCH:
                        second(u - 1)
                    unit(u)

            pe.wait_ge(w_in, 16 * 3)
            slots(pe, slot)



CT = 448
NCT = S // CT
HEADS, DH = 8, 32
HG = 2
HPG = HEADS // HG
NT = -(-S // P)
SCALE = DH ** -0.5
SHIFT = 5.0
ROT = DH // 2 + 1
NFK = ROT * DH + DH + 2
KH = ((0, 9 * DH), (9 * DH, NFK))
KX = DH + DH // 2
FLIN, FONE = ROT * DH, ROT * DH + DH
FT = 5
LASTK = 3 * DH + 1
HID = 4 * C
EARLY = NCT - 2
HT = HID // P
TOPK = S // 2 - 1
LN_EPS = 1e-5


def tile_rows(j):
    return min(P, S - j * P)


class Norm:

    def __init__(self, ctx, nc, tag, t, xn, avg, eps, banks):
        def sb(name, shape):
            return ctx.enter_context(nc.sbuf_tensor(name + tag, shape, F32))

        def sem(name):
            return ctx.enter_context(nc.semaphore(name + tag))

        self.t, self.xn, self.avg, self.eps = t, xn, avg, eps
        self.mean, self.mean_sq = banks[:, 0, 0:CT], banks[:, 1, 0:CT]
        self.sq = [sb(f"lsq{k}", [P, CH, CT]) for k in range(2)]
        self.m2 = [sb(f"lm2{k}", [P, CT]) for k in range(2)]
        self.var = [sb(f"lvar{k}", [P, CT]) for k in range(2)]
        self.s_sq_done = sem("s_sq_done")
        self.s_stat = sem("s_stat")
        self.s_m2_done = sem("s_m2_done")
        self.s_var_done = sem("s_var_done")
        self.s_std_done = sem("s_std_done")
        self.s_rstd = sem("s_rstd")
        self.s_cent = sem("s_cent")
        self.s_xn_done = sem("s_xn_done")

    def ch(self, c):
        return slice(c * CT, (c + 1) * CT)

    def until(self, eng, sem, n, c, back):
        v = n * NCT + (c - back if c >= 1 else 0)
        if not (isinstance(v, int) and v <= 0):
            eng.wait_ge(sem, v)

    def square(self, act, n, c):
        self.until(act, self.s_stat, n, c, 1)
        act.activation(self.sq[c % 2][:], self.t[:, :, self.ch(c)], ACT.Square).then_inc(self.s_sq_done, 1)

    def stats(self, pe, n, c):
        self.until(pe, self.s_var_done, n, c, 0)
        self.until(pe, self.s_cent, n, c, 0)
        for k in range(CH):
            pe.matmul(self.mean, self.avg[:], self.t[:, k, self.ch(c)], start=(k == 0), stop=(k == CH - 1))
        pe.wait_ge(self.s_sq_done, n * NCT + c + 1)
        for k in range(CH):
            mm = pe.matmul(self.mean_sq, self.avg[:], self.sq[c % 2][:, k, :], start=(k == 0), stop=(k == CH - 1))
        mm.then_inc(self.s_stat, 1)

    def mean2(self, act, n, c):
        act.wait_ge(self.s_stat, n * NCT + c + 1)
        act.activation(self.m2[c % 2][:], self.mean, ACT.Square).then_inc(self.s_m2_done, 1)

    def center(self, v, n, c):
        v.wait_ge(self.s_m2_done, n * NCT + c + 1)
        self.until(v, self.s_xn_done, n, c, 1)
        v.tensor_tensor(self.var[c % 2][:], self.mean_sq, self.m2[c % 2][:], ALU.subtract).then_inc(self.s_var_done, 1)
        v.tensor_tensor(self.xn[:, :, self.ch(c)], self.t[:, :, self.ch(c)],
                        self.mean.unsqueeze(1).broadcast_to([P, CH, CT]), ALU.subtract).then_inc(self.s_cent, 1)

    def std(self, act, n, c):
        act.wait_ge(self.s_var_done, n * NCT + c + 1)
        v = self.var[c % 2][:]
        act.activation(v, v, ACT.Sqrt, bias=self.eps[:]).then_inc(self.s_std_done, 1)

    def scale(self, v, n, c):
        i = n * NCT + c
        v.wait_ge(self.s_std_done, i + 1)
        r = self.var[c % 2]
        v.reciprocal(r[:], r[:]).then_inc(self.s_rstd, 1)
        v.wait_ge(self.s_rstd, i + 1)
        v.wait_ge(self.s_cent, i + 1)
        o = self.xn[:, :, self.ch(c)]
        v.tensor_tensor(o, o, r[:].unsqueeze(1).broadcast_to([P, CH, CT]), ALU.mult).then_inc(self.s_xn_done, 1)



def attention_stage(nc, x, conv_dram, t2_dram, wq, wkv, bk, bv, bq, projw, projb, sel_dram, selb_dram, heads_dram,
                    avg_dram, ident_dram, keep):
    ctx = ExitStack()
    with ctx:
        def sb(name, shape, dt=F32):
            return ctx.enter_context(nc.sbuf_tensor(name, shape, dt))

        def sem(name):
            return ctx.enter_context(nc.semaphore(name))

        ps = keep["ps"]
        t = sb("t", [P, CH, S])
        xn = sb("xn", [P, CH, S])
        qsp = sb("qsp", [P, 3, S], BF16)
        qst = sb("qst", [3 * DH, HPG, S], BF16)
        at = sb("at", [P, HG, S])
        wq_s = sb("wq_s", [P, CH, HG, P])
        wkv_s = sb("wkv_s", [P, CH, HG, HPG * KX + P])
        bk_s = sb("bk_s", [P, HG, HPG * KX])
        bv_s = sb("bv_s", [P, HG])
        bq_s = sb("bq_s", [P, HG])
        pw_s = sb("pw_s", [P, HG, C])
        pb_s = sb("pb_s", [P, CH])
        tout = sb("tout", [P, CH, CT])
        sel = sb("sel", [3 * DH, FT, P], BF16)
        selb = sb("selb", [P, 1])
        avg = sb("avg", [P, P])
        ident = sb("ident2", [P, P])
        heads = sb("heads", [P, P])
        nkeys = sb("nkeys", [P, 1])
        eps = sb("eps", [P, 1])
        kv = [sb(f"kv{k}", [P, HPG * KX + P]) for k in range(3)]
        phk = [sb(f"phk{k}", [P, HPG, NFK]) for k in range(2)]
        sn = sb("sn", [P, FT * P])
        sx = sb("sx", [P, ROT - 2, 2, DH])
        self32 = sx[0:3 * DH].rearrange("p r u i -> p (r u i)")[:, 0:FT * P].rearrange("p (f m) -> p f m", m=P)
        corr = [sb(f"corr{k}", [P, DH]) for k in range(3)]
        snt = sb("snt", [P, FT, P])
        gram = sb("gram", [P, HPG, DH])
        kbar = sb("kbar", [P, 1])
        qr = [sb(f"qr{k}", [P, CT]) for k in range(2)]
        phq = [sb(f"phq{k}", [P, HPG, CT]) for k in range(2)]
        qt = [sb(f"qt{k}", [P, CT]) for k in range(2)]
        rd = [sb(f"rd{k}", [P, CT]) for k in range(2)]
        norm = Norm(ctx, nc, "a", t, xn, avg, eps, ps[:, 6:8])

        avg_in = sem("avg_in2")
        w_in = sem("w_in2")
        ready0 = sem("ready0")
        sel_ready = sem("sel_ready")
        gate = sem("gate2")
        out_gate = sem("out_gate2")
        x_in = [sem(f"x_in2{c}") for c in range(NCT)]
        t2_out = [sem(f"t2_out{c}") for c in range(NCT)]
        tsum = sem("tsum")
        pb_mm = sem("pb_mm")
        pb_done = sem("pb_done")
        q_mm = sem("q_mm")
        qf_done = sem("qf_done")
        qh_done = sem("qh_done")
        qr_done = sem("qr_done")
        qm_done = sem("qm_done")
        ql_done = sem("ql_done")
        qst_in = sem("qst_in")
        kv_mm = sem("kv_mm")
        kv_done = sem("kv_done")
        v_done = sem("v_done")
        klin = sem("klin")
        phi = sem("phi")
        s_mm = sem("s_mm")
        sn_done = sem("sn_done")
        cor = sem("cor")
        gram_done = sem("gram_done")
        tr = sem("tr")
        snt_done = sem("snt_done")
        sel_mm = sem("sel_mm")
        phq_done = sem("phq_done")
        o_mm = sem("o_mm")
        t_mm = sem("t_mm")
        qt_done = sem("qt_done")
        den_mm = sem("den_mm")
        den_done = sem("den_done")
        rd_done = sem("rd_done")
        att = sem("att")
        p_mm = sem("p_mm")
        t2_done = sem("t2_done")
        x_v = x.rearrange("b (k p) s -> b p k s", p=P)
        conv_v = conv_dram.rearrange("b (k p) s -> b p k s", p=P)
        t2_v = t2_dram.rearrange("b (k p) s -> b p k s", p=P)
        NSN = 8
        NSEL = NCT * FT * 2

        def ch(c):
            return slice(c * CT, (c + 1) * CT)

        def query_bank(hg, c):
            return c % 2 if hg == 0 else 6 + c % 2

        def out_bank(hg, c):
            return 4 + 2 * (c % 2) if hg == 0 else 4

        block = ctx.enter_context(nc.Block())

        @block.gpsimd
        def _(pool):
            pool.dma_start(avg[:], avg_dram).then_inc(avg_in, 16)
            pool.memset(eps[:], LN_EPS).then_inc(ready0, 1)
            for out, src in ((wq_s, wq), (wkv_s, wkv), (bk_s, bk), (bv_s, bv), (bq_s, bq), (pw_s, projw), (pb_s, projb),
                             (selb, selb_dram), (heads, heads_dram), (ident, ident_dram)):
                pool.dma_start(out[:], src).then_inc(w_in, 16)
            pool.dma_start(self32, sel_dram).then_inc(w_in, 16)
            pool.memset(nkeys[:], SHIFT * SHIFT * S).then_inc(ready0, 1)
            for k in range(2):
                pool.memset(phk[k][:, :, FONE:FONE + 1], 1.0).then_inc(ready0, 1)
                pool.memset(phk[k][:, :, FONE + 1:NFK], 0.0).then_inc(ready0, 1)
        NW_IN = 16 * 11

        @block.sync
        def _(sp):
            def load_conv(b):
                for c in range(NCT):
                    sp.dma_start(xn[:, :, ch(c)], conv_v[bass.ds(b, 1), :, :, ch(c)]).then_inc(x_in[c], 16)

            def stack(b):
                for hg in range(HG):
                    sp.wait_ge(ql_done, b * HG * NCT + (hg + 1) * NCT)
                    sp.wait_ge(qm_done, b * HG * NCT + (hg + 1) * NCT)
                    if hg > 0:
                        sp.wait_ge(sel_mm, b * HG * NSEL + NSEL)
                    for f in range(3):
                        for h in range(HPG):
                            sp.dma_start(qst[32 * f:32 * f + 32, h, :], qsp[32 * h:32 * h + 32, f, :]).then_inc(qst_in, 16)

            def store(b, c):
                sp.wait_ge(t2_done, b * NCT * CH + (c + 1) * CH)
                sp.dma_start(t2_v[bass.ds(b, 1), :, :, ch(c)], tout[:]).then_inc(t2_out[c], 16)

            for c in range(NCT):
                sp.dma_start(t[:, :, ch(c)], x_v[0, :, :, ch(c)]).then_inc(x_in[c], 16)
                sp.dma_start(xn[:, :, ch(c)], conv_v[0, :, :, ch(c)]).then_inc(x_in[c], 16)
            with sp.Fori(0, B - 1) as b:
                stack(b)
                sp.wait_ge(kv_mm, (b + 1) * HG * NT)
                load_conv(b + 1)
                for c in range(NCT):
                    store(b, c)
                    sp.dma_start(t[:, :, ch(c)], x_v[bass.ds(b + 1, 1), :, :, ch(c)]).then_inc(x_in[c], 16)
                sp.wait_ge(t2_out[NCT - 1], 16 * (b + 1))
                sp.sem_inc(out_gate, 1)
            stack(B - 1)
            for c in range(NCT):
                store(B - 1, c)
            for c in range(NCT):
                sp.wait_ge(t2_out[c], 16 * B)

        @block.scalar
        def _(act):
            def square(n, c):
                act.wait_ge(tsum, n * NCT + c + 1)
                norm.square(act, n, c)

            def queries(b, hg):
                if hg == 0:
                    square(b, EARLY)
                for c in range(NCT):
                    n = b * HG * NCT + hg * NCT + c
                    bank = ps[:, query_bank(hg, c), 0:CT]
                    act.wait_ge(q_mm, n + 1)
                    if hg > 0 and c == 0:
                        act.wait_ge(qst_in, 16 * (b * HG * 3 * HPG + 3 * HPG))
                    act.activation(at[:, hg, ch(c)], bank, ACT.Identity, bias=bq_s[:, hg:hg + 1]).then_inc(qf_done, 1)
                    act.activation(qsp[:, 0, ch(c)], bank, ACT.Identity, bias=bq_s[:, hg:hg + 1]).then_inc(qh_done, 1)
                    if c >= 1:
                        middle(b, hg, c - 1)
                    if hg == 0:
                        if c == 1:
                            norm.mean2(act, b, EARLY)
                        if c == 2:
                            norm.std(act, b, EARLY)
                            square(b, EARLY + 1)
                        if c == 3:
                            norm.mean2(act, b, EARLY + 1)
                        if c == 4:
                            norm.std(act, b, EARLY + 1)
                middle(b, hg, NCT - 1)

            def middle(b, hg, c):
                act.wait_ge(qr_done, b * HG * NCT + hg * NCT + c + 1)
                act.activation(qsp[:, 1, ch(c)], qr[c % 2][:], ACT.Copy).then_inc(qm_done, 1)

            def keys(b, hg):
                for j in range(NT):
                    n = b * HG * NT + hg * NT + j
                    r = tile_rows(j)
                    ki = kv[j % 3][0:r, 0:HPG * KX].rearrange("p (h i) -> p h i", i=KX)[:, :, 0:DH]
                    act.wait_ge(kv_done, n + 1)
                    if j >= 3:
                        act.wait_ge(s_mm, n - 2)
                    act.activation(kv[j % 3][0:r, HPG * KX:], ps[0:r, 4 + j % 2, HPG * KX:HPG * KX + P], ACT.Copy).then_inc(v_done, 1)
                    if j >= 2:
                        act.wait_ge(s_mm, n - 1)
                    act.activation(phk[j % 2][0:r, :, 0:DH], ki, ACT.Square).then_inc(klin, 1)
                    act.activation(phk[j % 2][0:r, :, FLIN:FLIN + DH], ki, ACT.Copy).then_inc(klin, 1)

            def sums(b, hg):
                act.wait_ge(s_mm, b * HG * NT + (hg + 1) * NT)
                s2, s1 = SCALE * SCALE, 2 * SHIFT * SCALE / 4
                lo, hi = ps[:, 0, :], ps[:, 1, :]
                f0 = KH[1][0]
                r16, lin, one = 4 * P - f0, FLIN - f0, FONE - f0
                for dst, width, src, f in (
                    (0, f0, lo[:, 0:f0], s2),
                    (f0, r16, hi[:, 0:r16], s2),
                    (4 * P, DH, hi[:, r16:r16 + DH], s2 / 2),
                    (4 * P + DH, DH, hi[:, lin:lin + DH], s1),
                    (4 * P + 2 * DH, DH, hi[:, lin:lin + DH], -s1),
                    (4 * P + 3 * DH, 1, hi[:, one:one + 1], SHIFT * SHIFT),
                ):
                    act.activation(sn[:, dst:dst + width], src, ACT.Copy, scale=f).then_inc(sn_done, 1)
                for r0, n, src in ((0, 8, lo[:, DH:f0]), (8, 7, hi[:, 0:r16])):
                    act.activation(sx[:, r0:r0 + n], src.rearrange("p (r i) -> p r i", i=DH).unsqueeze(2).broadcast_to([P, n, 2, DH]),
                                   ACT.Copy, scale=s2).then_inc(sn_done, 1)

            def squares(b, hg, more):
                for c in range(NCT):
                    for f in range(FT):
                        for hp in range(2):
                            n = (c * FT + f) * 2 + hp
                            act.wait_ge(sel_mm, b * HG * NSEL + hg * NSEL + n + 1)
                            k = c * FT + f
                            if k >= 2 and hp == 0:
                                act.wait_ge(o_mm, b * HG * NCT * FT + hg * NCT * FT + k - 1)
                            src = ps[:, 2 * hp:2 * hp + 2, 0:CT]
                            dst = phq[k % 2][:, 2 * hp:2 * hp + 2, :]
                            if f < FT - 1:
                                act.activation(dst, src, ACT.Square).then_inc(phq_done, 1)
                            else:
                                act.activation(dst, src, ACT.Square, bias=selb[:]).then_inc(phq_done, 1)
                        beside = more and hg == 1 and c >= 2
                        if f == 0:
                            n = b * HG * NCT + hg * NCT + c
                            act.wait_ge(den_mm, n + 1)
                            if c >= 2:
                                act.wait_ge(att, n - 1)
                            act.activation(rd[c % 2][:], ps[:, 5, 0:CT], ACT.Identity, bias=nkeys[:]).then_inc(den_done, 1)
                        if beside and f == 0:
                            square(b + 1, c - 2)
                        if beside and f == 1:
                            norm.mean2(act, b + 1, c - 2)
                        if beside and f == 2:
                            norm.std(act, b + 1, c - 2)

            act.wait_ge(ready0, 1)
            def body(b, more):
                queries(b, 0)
                for hg in range(HG):
                    keys(b, hg)
                    sums(b, hg)
                    if hg == 0:
                        queries(b, 1)
                    squares(b, hg, more)

            square(0, 0)
            for c in range(EARLY):
                if c + 1 < EARLY:
                    square(0, c + 1)
                norm.mean2(act, 0, c)
                norm.std(act, 0, c)
            act.wait_ge(ready0, 6)
            act.wait_ge(w_in, NW_IN)
            with act.Fori(0, B - 1) as b:
                body(b, True)
            body(B - 1, False)

        @block.vector
        def _(v):
            def residual(n, c):
                v.wait_ge(x_in[c], 32 * (n + 1))
                v.tensor_tensor(t[:, :, ch(c)], t[:, :, ch(c)], xn[:, :, ch(c)], ALU.add).then_inc(tsum, 1)

            def join(b, c):
                if c >= 1:
                    v.wait_ge(t2_out[c - 1], 16 * (b + 1))
                for h in range(CH):
                    v.wait_ge(p_mm, b * NCT * CH + c * CH + h + 1)
                    v.scalar_tensor_tensor(tout[:, h], ps[:, 6 + h, 0:CT], pb_s[:, h:h + 1], t[:, h, ch(c)], ALU.add, ALU.add).then_inc(t2_done, 1)

            def queries(b, hg):
                def low(c):
                    v.wait_ge(qm_done, b * HG * NCT + hg * NCT + c + 1)
                    v.tensor_tensor(qsp[:, 2, ch(c)], qr[c % 2][:], qsp[:, 1, ch(c)], ALU.subtract).then_inc(ql_done, 1)
                for c in range(NCT):
                    v.wait_ge(qh_done, b * HG * NCT + hg * NCT + c + 1)
                    if c >= 2:
                        v.wait_ge(ql_done, b * HG * NCT + hg * NCT + c - 1)
                    v.tensor_tensor(qr[c % 2][:], at[:, hg, ch(c)], qsp[:, 0, ch(c)], ALU.subtract).then_inc(qr_done, 1)
                    low(c)
                    if hg == 1 and c == 3:
                        turned(b, 0)
                    if hg == 0:
                        if c == 1:
                            residual(b, EARLY + 1)
                            norm.center(v, b, EARLY)
                        if c == 2:
                            norm.scale(v, b, EARLY)
                        if c == 3:
                            norm.center(v, b, EARLY + 1)
                            norm.scale(v, b, EARLY + 1)

            def keys(b, hg):
                def evacuate(j):
                    n = b * HG * NT + hg * NT + j
                    r = tile_rows(j)
                    v.wait_ge(kv_mm, n + 1)
                    if j >= 3:
                        v.wait_ge(s_mm, n - 2)
                        v.wait_ge(klin, 2 * (n - 2))
                    v.tensor_tensor(kv[j % 3][0:r, 0:HPG * KX], ps[0:r, 4 + j % 2, 0:HPG * KX], bk_s[0:r, hg, :],
                                    ALU.add).then_inc(kv_done, 1)

                evacuate(0)
                for j in range(NT):
                    n = b * HG * NT + hg * NT + j
                    r = tile_rows(j)
                    if j + 1 < NT:
                        evacuate(j + 1)
                    ki = kv[j % 3][0:r, 0:HPG * KX].rearrange("p (h i) -> p h i", i=KX)[:, :, 0:DH]
                    v.wait_ge(kv_done, n + 1)
                    if j >= 2:
                        v.wait_ge(s_mm, n - 1)
                    kr = bass.AP(ki.tensor, ki.offset + 1, [ki.ap[0], ki.ap[1], [1, ROT - 1], [1, DH]])
                    v.tensor_tensor(phk[j % 2][0:r, :, DH:FLIN].rearrange("p h (r i) -> p h r i", i=DH),
                                    ki.unsqueeze(2).broadcast_to([r, HPG, ROT - 1, DH]), kr, ALU.mult).then_inc(phi, 1)

            def corrections(b, hg):
                m = b * HG + hg
                v.wait_ge(s_mm, (m + 1) * NT)
                v.scalar_tensor_tensor(gram[:], ps[:, 2, 0:DH].unsqueeze(1).broadcast_to([P, HPG, DH]),
                                       SCALE * SCALE, heads[:].rearrange("p (h i) -> p h i", i=DH),
                                       ALU.mult, ALU.mult).then_inc(gram_done, 1)
                v.tensor_scalar(kbar[:], ps[:, 2, DH:DH + 1], 2 * SHIFT * SCALE, None, ALU.mult).then_inc(gram_done, 1)
                v.wait_ge(sn_done, NSN * (m + 1))
                v.tensor_reduce(corr[0][:], sn[:, DH:4 * P].rearrange("p (r i) -> p i r", i=DH), AX.X, ALU.add).then_inc(cor, 1)
                a = sx[:]
                back = bass.AP(a.tensor, a.offset + DH - 1, [a.ap[0], [1, DH], [2 * DH - 1, ROT - 2]])
                v.tensor_reduce(corr[1][:], back, AX.X, ALU.add).then_inc(cor, 1)
                v.scalar_tensor_tensor(corr[2][:], sn[:, 4 * P:4 * P + DH], -2.0, sn[:, 0:DH], ALU.mult, ALU.add).then_inc(cor, 1)
                v.wait_ge(cor, 5 * m + 3)
                v.tensor_tensor(corr[0][:], corr[0][:], corr[1][:], ALU.add).then_inc(cor, 1)
                v.wait_ge(cor, 5 * m + 4)
                v.tensor_tensor(sn[:, 0:DH], corr[2][:], corr[0][:], ALU.subtract).then_inc(cor, 1)

            def turned(b, hg):
                m = b * HG + hg
                v.wait_ge(tr, 2 * m + 2)
                v.tensor_copy(snt[:, 0:4, :], ps[:, 4, :].rearrange("p (f m) -> p f m", m=P)).then_inc(snt_done, 1)
                v.tensor_copy(snt[0:LASTK, 4, :], ps[0:LASTK, 5, 0:P]).then_inc(snt_done, 1)

            def outputs(b, hg, more):
                def weigh(c):
                    n = b * HG * NCT + hg * NCT + c
                    v.wait_ge(t_mm, n + 1)
                    if c >= 2:
                        v.wait_ge(den_mm, n - 1)
                    v.scalar_tensor_tensor(qt[c % 2][:], ps[:, 5, 0:CT], kbar[:], at[:, hg, ch(c)], ALU.add, ALU.mult).then_inc(qt_done, 1)

                v.wait_ge(gram_done, 2 * (b * HG + hg) + 2)
                weigh(0)
                for c in range(NCT):
                    n = b * HG * NCT + hg * NCT + c
                    beside = more and hg == 1 and c >= 2
                    if beside:
                        residual(b + 1, c - 2)
                    v.wait_ge(den_done, n + 1)
                    v.reciprocal(rd[c % 2][:], rd[c % 2][:]).then_inc(rd_done, 1)
                    if beside:
                        norm.center(v, b + 1, c - 2)
                    if c + 1 < NCT:
                        weigh(c + 1)
                    if beside:
                        norm.scale(v, b + 1, c - 2)
                    if hg == 1 and c >= 1:
                        join(b, c - 1)
                    v.wait_ge(rd_done, n + 1)
                    v.wait_ge(qt_done, n + 1)
                    v.wait_ge(o_mm, b * HG * NCT * FT + hg * NCT * FT + (c + 1) * FT)
                    v.tensor_tensor(at[:, hg, ch(c)], ps[:, out_bank(hg, c), 0:CT], rd[c % 2][:], ALU.mult).then_inc(att, 1)

            def body(b, more):
                residual(b, EARLY)
                queries(b, 0)
                for hg in range(HG):
                    keys(b, hg)
                    corrections(b, hg)
                    if hg == 0:
                        queries(b, 1)
                    else:
                        turned(b, 1)
                    outputs(b, hg, more)
                join(b, NCT - 1)

            for c in range(EARLY):
                residual(0, c)
            for c in range(EARLY):
                norm.center(v, 0, c)
                norm.scale(v, 0, c)
            v.wait_ge(w_in, NW_IN)
            v.wait_ge(ready0, 6)
            v.tensor_copy(sel[:], self32).then_inc(sel_ready, 1)
            v.wait_ge(pb_mm, 1)
            v.tensor_tensor(pb_s[:], pb_s[:], ps[:, 0, 0:CH], ALU.add).then_inc(pb_done, 1)
            v.wait_ge(pb_done, 1)
            with v.Fori(0, B - 1) as b:
                body(b, True)
            body(B - 1, False)

        @block.tensor
        def _(pe):
            def stats(n, c):
                pe.wait_ge(tsum, n * NCT + c + 1)
                norm.stats(pe, n, c)

            def project_out(b, c):
                pe.wait_ge(att, b * HG * NCT + NCT + c + 1)
                if c >= 1:
                    pe.wait_ge(t2_done, b * NCT * CH + c * CH)
                for h in range(CH):
                    for k in range(HG):
                        mm = pe.matmul(ps[:, 6 + h, 0:CT], pw_s[:, k, h * P:(h + 1) * P], at[:, k, ch(c)],
                                       start=(k == 0), stop=(k == HG - 1))
                    mm.then_inc(p_mm, 1)

            def queries(b, hg):
                for c in range(NCT):
                    n = b * HG * NCT + hg * NCT + c
                    if hg == 0:
                        pe.wait_ge(norm.s_xn_done, b * NCT + c + 1)
                    if c >= 2:
                        pe.wait_ge(qh_done, n - 1)
                    for k in range(CH):
                        mm = pe.matmul(ps[:, query_bank(hg, c), 0:CT], wq_s[:, k, hg, :], xn[:, k, ch(c)], start=(k == 0), stop=(k == CH - 1))
                    mm.then_inc(q_mm, 1)
                    if hg == 1 and c == 4:
                        turn(b, 0)
                    if hg == 0 and c in (1, 3):
                        stats(b, EARLY + c // 2)

            def keys(b, hg):
                def project(j):
                    n = b * HG * NT + hg * NT + j
                    r = tile_rows(j)
                    if j >= 2:
                        pe.wait_ge(kv_done, n - 1)
                        pe.wait_ge(v_done, n - 1)
                    for k in range(CH):
                        mm = pe.matmul(ps[0:r, 4 + j % 2, 0:HPG * KX + P], xn[:, k, j * P:j * P + r], wkv_s[:, k, hg, :],
                                       start=(k == 0), stop=(k == CH - 1))
                    mm.then_inc(kv_mm, 1)

                project(0)
                project(1)
                for j in range(NT):
                    n = b * HG * NT + hg * NT + j
                    r = tile_rows(j)
                    if j + 2 < NT:
                        project(j + 2)
                    pe.wait_ge(klin, 2 * (n + 1))
                    pe.wait_ge(phi, n + 1)
                    if r < P:
                        pe.sem_inc(gate, 1)
                    for f, (lo, hi) in enumerate(KH):
                        for h in range(HPG):
                            v0 = HPG * KX + DH * h
                            pe.matmul(ps[DH * h:DH * h + DH, f, 0:hi - lo], kv[j % 3][0:r, v0:v0 + DH],
                                      phk[j % 2][0:r, h, lo:hi], start=(j == 0), stop=(j == NT - 1))
                    for h in range(HPG):
                        mm = pe.matmul(ps[DH * h:DH * h + DH, 2, 0:DH + 1], kv[j % 3][0:r, KX * h:KX * h + DH],
                                       phk[j % 2][0:r, h, FLIN:FLIN + DH + 1], start=(j == 0), stop=(j == NT - 1))
                    mm.then_inc(s_mm, 1)

            def turn(b, hg):
                pe.wait_ge(cor, 5 * (b * HG + hg) + 5)
                for f in range(4):
                    mm = pe.transpose(ps[:, 4, f * P:(f + 1) * P], sn[:, f * P:(f + 1) * P], ident[:])
                mm.then_inc(tr, 1)
                pe.transpose(ps[0:LASTK, 5, 0:P], sn[:, 4 * P:4 * P + LASTK], ident[:]).then_inc(tr, 1)

            def outputs(b, hg, more):
                def select(n):
                    k, hp = n // 2, n % 2
                    c, f = k // FT, k % FT
                    if n >= 2:
                        pe.wait_ge(phq_done, b * HG * NSEL + hg * NSEL + n - 1)
                    for h in (2 * hp, 2 * hp + 1):
                        mm = pe.matmul(ps[:, h, 0:CT], sel[:, f, :], qst[:, h, ch(c)], start=True, stop=True)
                    mm.then_inc(sel_mm, 1)

                pe.wait_ge(qst_in, 16 * 3 * HPG * (b * HG + hg + 1))
                pe.wait_ge(snt_done, 2 * (b * HG + hg + 1))
                pe.wait_ge(gram_done, 2 * (b * HG + hg + 1))
                def gram_q(c):
                    n = b * HG * NCT + hg * NCT + c
                    if c >= 1:
                        pe.wait_ge(den_done, n)
                    pe.matmul(ps[:, 5, 0:CT], gram[:].rearrange("p h i -> p (h i)"), at[:, hg, ch(c)], start=True, stop=True).then_inc(t_mm, 1)

                def denominators(c):
                    pe.wait_ge(qt_done, b * HG * NCT + hg * NCT + c + 1)
                    pe.matmul(ps[:, 5, 0:CT], heads[:], qt[c % 2][:], start=True, stop=True).then_inc(den_mm, 1)

                select(0)
                select(1)
                gram_q(0)
                denominators(0)
                for k in range(NCT * FT):
                    c, f = k // FT, k % FT
                    if k + 1 < NCT * FT:
                        select(2 * k + 2)
                        select(2 * k + 3)
                    pe.wait_ge(phq_done, b * HG * NSEL + hg * NSEL + 2 * k + 2)
                    n = b * HG * NCT + hg * NCT + c
                    if f == 0 and c >= 2 - hg:
                        pe.wait_ge(att, n - 1 + hg)
                    kr = P if f < FT - 1 else LASTK
                    for h in range(HPG):
                        mm = pe.matmul(ps[DH * h:DH * h + DH, out_bank(hg, c), 0:CT], snt[0:kr, f, DH * h:DH * h + DH],
                                       phq[k % 2][0:kr, h, :], start=(f == 0), stop=(f == FT - 1))
                    mm.then_inc(o_mm, 1)
                    if hg == 1 and more and c >= 2 and f == 0:
                        pe.wait_ge(t2_done, b * NCT * CH + (c - 1) * CH)
                        stats(b + 1, c - 2)
                    if f == 1 and c + 1 < NCT:
                        gram_q(c + 1)
                    if f == 3 and c + 1 < NCT:
                        denominators(c + 1)
                    if hg == 1 and f == 1 and c >= 1:
                        if more and c >= 2:
                            pe.wait_ge(norm.s_cent, (b + 1) * NCT + c - 1)
                        project_out(b, c - 1)

            def body(b, more):
                queries(b, 0)
                for hg in range(HG):
                    if hg > 0:
                        pe.wait_ge(att, b * HG * NCT + NCT)
                    keys(b, hg)
                    if hg == 0:
                        queries(b, 1)
                    else:
                        turn(b, 1)
                    outputs(b, hg, more)
                if more:
                    pe.wait_ge(norm.s_cent, (b + 1) * NCT + EARLY)
                project_out(b, NCT - 1)

            pe.wait_ge(avg_in, 16)
            for c in range(EARLY):
                stats(0, c)
            pe.wait_ge(w_in, NW_IN)
            pe.wait_ge(ready0, 6)
            pe.wait_ge(sel_ready, 1)
            for h in range(CH):
                for k in range(HG):
                    mm = pe.matmul(ps[:, 0, h:h + 1], pw_s[:, k, h * P:(h + 1) * P], bv_s[:, k:k + 1], start=(k == 0), stop=(k == HG - 1))
            mm.then_inc(pb_mm, 1)
            pe.wait_ge(pb_done, 1)
            with pe.Fori(0, B - 1) as b:
                body(b, True)
            body(B - 1, False)


LEAD = NCT - 1


def tie_pieces(c):
    return [(j, max(j * P, c * CT), min(j * P + tile_rows(j), (c + 1) * CT)) for j in range(NT)
            if max(j * P, c * CT) < min(j * P + tile_rows(j), (c + 1) * CT)]


def sums(c):
    return 13 if c == 0 else 7


def routed_stage(nc, t2_dram, out, wr, br, w1, b1, w2, b2, avg_dram, ident_dram, tri_dram, keep):
    ctx = ExitStack()
    with ctx:
        def sb(name, shape, dt=F32):
            return ctx.enter_context(nc.sbuf_tensor(name, shape, dt))

        def sem(name):
            return ctx.enter_context(nc.semaphore(name))

        ps = keep["ps"]
        t = sb("t3", [P, CH, S])
        xn = sb("xn3", [P, CH, S])
        wrow = sb("wrow", [P, S])
        wcol = sb("wcol", [P, NT])
        beats = sb("beats", [P, sums(0), CT], BF16)
        ties = [sb(f"ties{k}", [P, P]) for k in range(max(len(tie_pieces(c)) for c in range(NCT)))]
        ybuf = [sb(f"ybuf{k}", [P, CT]) for k in range(CH)]
        hid = [sb(f"hid{k}", [P, HT, CT]) for k in range(2)]
        w1_s = sb("w1_s", [P, CH, HID])
        w2_s = sb("w2_s", [P, HT, C])
        b1_s = sb("b1_s", [P, HT])
        b2_s = sb("b2_s", [P, CH])
        wr_s = sb("wr_s", [P, CH])
        wrb = sb("wrb", [P, CH, P])
        br_s = sb("br_s", [P, 1])
        avg = sb("avg3", [P, P])
        ident = sb("ident3", [P, P])
        tri = sb("tri", [P, P])
        ones = sb("ones3", [P, P], BF16)
        eps = sb("eps3", [P, 1])
        norm = Norm(ctx, nc, "f", t, xn, avg, eps, ps[:, 4:6])

        first_in = sem("first_in3")
        w_in = sem("w_in3")
        ready0 = sem("ready3")
        wrb_ready = sem("wrb_ready")
        gate = sem("gate3")
        t_in = [sem(f"t_in{c}") for c in range(NCT)]
        out_st = [sem(f"out_st{c}") for c in range(NCT)]
        r_mm = sem("r_mm")
        r_done = sem("r_done")
        wc_mm = sem("wc_mm")
        wc_done = sem("wc_done")
        bt_tie = sem("bt_tie")
        bt_sum = sem("bt_sum")
        bt_done = sem("bt_done")
        rk_mm = sem("rk_mm")
        mw = sem("mw")
        up_mm = sem("up_mm")
        gelu = sem("gelu")
        dn_mm = sem("dn_mm")
        ysc = sem("ysc")
        yxn = sem("yxn")
        fin = sem("fin")
        t2_v = t2_dram.rearrange("b (k p) s -> b p k s", p=P)
        out_v = out.rearrange("b (k p) s -> b p k s", p=P)

        def ch(c):
            return slice(c * CT, (c + 1) * CT)

        block = ctx.enter_context(nc.Block())

        @block.gpsimd
        def _(pool):
            pool.memset(ones[:], 1.0).then_inc(ready0, 1)
            pool.memset(eps[:], LN_EPS).then_inc(ready0, 1)
            for o, src in ((avg, avg_dram), (wr_s, wr), (br_s, br)):
                pool.dma_start(o[:], src).then_inc(first_in, 16)
            for o, src in ((b1_s, b1), (w1_s, w1), (ident, ident_dram), (tri, tri_dram), (w2_s, w2), (b2_s, b2)):
                pool.dma_start(o[:], src).then_inc(w_in, 16)
        NW_IN = 16 * 6

        @block.sync
        def _(sp):
            def store(b, c):
                sp.wait_ge(fin, b * NCT * CH + (c + 1) * CH)
                sp.dma_start(out_v[bass.ds(b, 1), :, :, ch(c)], t[:, :, ch(c)]).then_inc(out_st[c], 16)

            def load(b, c):
                sp.dma_start(t[:, :, ch(c)], t2_v[bass.ds(b, 1), :, :, ch(c)]).then_inc(t_in[c], 16)

            for c in range(NCT):
                load(0, c)
            with sp.Fori(0, B - 1) as b:
                for c in range(NCT):
                    store(b, c)
                    sp.wait_ge(out_st[c], 16 * (b + 1))
                    load(b + 1, c)
            for c in range(NCT):
                store(B - 1, c)
            for c in range(NCT):
                sp.wait_ge(out_st[c], 16 * B)

        @block.scalar
        def _(act):
            def square(n, c):
                act.wait_ge(t_in[c], 16 * (n + 1))
                norm.square(act, n, c)

            def deviation(n, c):
                square(n, c)
                norm.mean2(act, n, c)
                norm.std(act, n, c)

            def weigh(n, c):
                act.wait_ge(r_mm, n * NCT + c + 1)
                act.activation(wrow[:, ch(c)], ps[:, 6, 0:CT], ACT.Identity, bias=br_s[:]).then_inc(r_done, 1)

            def hidden(b, c, hs):
                for h in hs:
                    n = c * HT + h
                    act.wait_ge(up_mm, b * NCT * HT + n + 1)
                    act.activation(hid[c % 2][:, h, :], ps[:, n % 2, 0:CT], ACT.Gelu_apprx_tanh,
                                   bias=b1_s[:, h:h + 1]).then_inc(gelu, 1)

            def body(b, more):
                hidden(b, 0, range(2))
                weigh(b, LEAD - 1)
                hidden(b, 0, range(2, 5))
                deviation(b, LEAD)
                hidden(b, 0, range(5, HT))
                hidden(b, 1, range(1))
                weigh(b, LEAD)
                hidden(b, 1, range(1, HT))
                for c in range(2, NCT):
                    hidden(b, c, range(HT // 2))
                    if more and c >= 3:
                        weigh(b + 1, c - 3)
                    hidden(b, c, range(HT // 2, HT))
                    if more:
                        deviation(b + 1, c - 2)
                if more:
                    weigh(b + 1, LEAD - 2)
                    deviation(b + 1, LEAD - 1)

            act.wait_ge(first_in, 48)
            act.wait_ge(ready0, 2)
            square(0, 0)
            for c in range(LEAD):
                if c + 1 < LEAD:
                    square(0, c + 1)
                norm.mean2(act, 0, c)
                norm.std(act, 0, c)
                if c < LEAD - 1:
                    weigh(0, c)
            act.wait_ge(w_in, NW_IN)
            with act.Fori(0, B - 1) as b:
                body(b, True)
            body(B - 1, False)

        @block.vector
        def _(v):
            def columns(b):
                rl = tile_rows(NT - 1)
                v.wait_ge(wc_mm, b + 1)
                v.tensor_copy(wcol[:, 0:NT - 1], ps[:, 7, 0:NT - 1]).then_inc(wc_done, 1)
                v.tensor_copy(wcol[0:rl, NT - 1:NT], ps[0:rl, 7, NT - 1:NT]).then_inc(wc_done, 1)
                v.wait_ge(wc_done, 2 * b + 2)

            def compare(b, c, part):
                if part == 0 and c > 0:
                    v.wait_ge(rk_mm, b * NCT + c)
                c0, c1 = c * CT, (c + 1) * CT
                for k, (j, lo, hi) in enumerate(tie_pieces(c) if part == 0 else ()):
                    r = tile_rows(j)
                    v.scalar_tensor_tensor(ties[k][0:r, 0:hi - lo], wrow[0:r, lo:hi], wcol[0:r, j:j + 1],
                                           tri[0:r, lo - j * P:hi - j * P], ALU.is_equal, ALU.mult).then_inc(bt_tie, 1)
                done = (b * NCT + c) * NT
                for j in PARTS[part]:
                    r, g = tile_rows(j), j % sums(c)
                    mid = min(max(j * P + r, c0), c1)
                    if j >= sums(c):
                        v.wait_ge(bt_sum, done + j - sums(c) + 1)
                    for lo, hi, cmp in ((c0, mid, ALU.is_lt), (mid, c1, ALU.is_le)):
                        if lo < hi:
                            o = beats[0:r, g, lo - c0:hi - c0]
                            if j < sums(c):
                                op = v.tensor_scalar(o, wrow[0:r, lo:hi], wcol[0:r, j:j + 1], None, cmp)
                            else:
                                op = v.scalar_tensor_tensor(o, wrow[0:r, lo:hi], wcol[0:r, j:j + 1], o, cmp, ALU.add)
                    op.then_inc(bt_sum, 1)
                if part < len(PARTS) - 1:
                    return
                v.wait_ge(bt_sum, done + NT)
                v.wait_ge(bt_tie, b * TIES + sum(len(tie_pieces(x)) for x in range(c + 1)))
                for k, (j, lo, hi) in enumerate(tie_pieces(c)):
                    r, g = tile_rows(j), j % sums(c)
                    o = beats[0:r, g, lo - c0:hi - c0]
                    op = v.tensor_tensor(o, o, ties[k][0:r, 0:hi - lo], ALU.add)
                op.then_inc(bt_done, 1)

            def mask(b, c):
                v.wait_ge(rk_mm, b * NCT + c + 1)
                v.scalar_tensor_tensor(wrow[:, ch(c)], ps[:, 7, 0:CT], TOPK - 0.5, wrow[:, ch(c)],
                                       ALU.is_lt, ALU.mult).then_inc(mw, 1)

            def finish(b, c):
                v.wait_ge(mw, b * NCT + c + 1)
                for h in range(CH):
                    n = b * NCT * CH + c * CH + h
                    v.wait_ge(dn_mm, n + 1)
                    y = ybuf[h]
                    v.scalar_tensor_tensor(y[:], ps[:, 2 + h, 0:CT], b2_s[:, h:h + 1], wrow[:, ch(c)],
                                           ALU.add, ALU.mult).then_inc(ysc, 1)
                    o = t[:, h, ch(c)]
                    v.tensor_tensor(o, o, xn[:, h, ch(c)], ALU.add).then_inc(yxn, 1)
                    v.wait_ge(ysc, n + 1)
                    v.wait_ge(yxn, n + 1)
                    v.tensor_tensor(o, o, y[:], ALU.add).then_inc(fin, 1)

            def body(b, more):
                norm.center(v, b, LEAD)
                norm.scale(v, b, LEAD)
                columns(b)
                for part in range(3):
                    compare(b, 0, part)
                mask(b, 0)
                for c in range(NCT - 1):
                    compare(b, c + 1, 0)
                    if more and c >= 1:
                        norm.center(v, b + 1, c - 1)
                    compare(b, c + 1, 1)
                    if more and c >= 1:
                        norm.scale(v, b + 1, c - 1)
                    if c == NCT - 2:
                        finish(b, c)
                    compare(b, c + 1, 2)
                    if c < NCT - 2:
                        finish(b, c)
                    mask(b, c + 1)
                if more:
                    norm.center(v, b + 1, LEAD - 1)
                    norm.scale(v, b + 1, LEAD - 1)
                finish(b, NCT - 1)

            PARTS = (range(14), range(14, 20), range(20, NT))
            TIES = sum(len(tie_pieces(c)) for c in range(NCT))
            v.wait_ge(first_in, 48)
            v.tensor_copy(wrb[:], wr_s[:].unsqueeze(2).broadcast_to([P, CH, P])).then_inc(wrb_ready, 1)
            for c in range(LEAD):
                norm.center(v, 0, c)
                norm.scale(v, 0, c)
            v.wait_ge(w_in, NW_IN)
            with v.Fori(0, B - 1) as b:
                body(b, True)
            body(B - 1, False)

        @block.tensor
        def _(pe):
            def stats(n, c):
                pe.wait_ge(t_in[c], 16 * (n + 1))
                norm.stats(pe, n, c)

            def router(n, c):
                pe.wait_ge(norm.s_xn_done, n * NCT + c + 1)
                norm.until(pe, r_done, n, c, 0)
                for k in range(CH):
                    mm = pe.matmul(ps[:, 6, 0:CT], wrb[:, k, :], xn[:, k, ch(c)], start=(k == 0), stop=(k == CH - 1))
                mm.then_inc(r_mm, 1)

            def columns(b):
                pe.wait_ge(r_done, (b + 1) * NCT)
                pe.sem_inc(gate, 1)
                for j in range(NT):
                    r = tile_rows(j)
                    mm = pe.transpose(ps[0:r, 7, j:j + 1], wrow[0:1, j * P:j * P + r], ident[0:1, 0:1])
                mm.then_inc(wc_mm, 1)

            def up(b, c, hs):
                for h in hs:
                    n = c * HT + h
                    if n >= 2:
                        pe.wait_ge(gelu, b * NCT * HT + n - 1)
                    for k in range(CH):
                        mm = pe.matmul(ps[:, n % 2, 0:CT], w1_s[:, k, h * P:(h + 1) * P], xn[:, k, ch(c)],
                                       start=(k == 0), stop=(k == CH - 1))
                    mm.then_inc(up_mm, 1)

            def rank(b, c):
                pe.wait_ge(bt_done, b * NCT + c + 1)
                if c > 0:
                    pe.wait_ge(mw, b * NCT + c)
                for g in range(sums(c)):
                    mm = pe.matmul(ps[:, 7, 0:CT], ones[:], beats[:, g, :], start=(g == 0), stop=(g == sums(c) - 1))
                mm.then_inc(rk_mm, 1)

            def down(b, c, h):
                n = c * CH + h
                if h == 0:
                    pe.wait_ge(gelu, b * NCT * HT + (c + 1) * HT)
                if n >= 2:
                    pe.wait_ge(ysc, b * NCT * CH + n - 1)
                for k in range(HT):
                    mm = pe.matmul(ps[:, 2 + h, 0:CT], w2_s[:, k, h * P:(h + 1) * P], hid[c % 2][:, k, :],
                                   start=(k == 0), stop=(k == HT - 1))
                mm.then_inc(dn_mm, 1)

            def body(b, more):
                up(b, 0, range(2))
                router(b, LEAD - 1)
                up(b, 0, range(2, 5))
                stats(b, LEAD)
                up(b, 0, range(5, HT))
                up(b, 1, range(1))
                router(b, LEAD)
                columns(b)
                up(b, 1, range(1, HT))
                down(b, 0, 0)
                rank(b, 0)
                down(b, 0, 1)
                for c in range(2, NCT):
                    up(b, c, range(HT // 2))
                    if more and c >= 3:
                        router(b + 1, c - 3)
                    up(b, c, range(HT // 2, HT))
                    rank(b, c - 1)
                    down(b, c - 1, 0)
                    if more:
                        stats(b + 1, c - 2)
                    down(b, c - 1, 1)
                if more:
                    router(b + 1, LEAD - 2)
                down(b, NCT - 1, 0)
                rank(b, NCT - 1)
                if more:
                    stats(b + 1, LEAD - 1)
                down(b, NCT - 1, 1)

            pe.wait_ge(first_in, 48)
            pe.wait_ge(ready0, 2)
            pe.wait_ge(wrb_ready, 1)
            stats(0, 0)
            for c in range(LEAD - 1):
                stats(0, c + 1)
                router(0, c)
            pe.wait_ge(w_in, NW_IN)
            with pe.Fori(0, B - 1) as b:
                body(b, True)
            body(B - 1, False)


def conv_arrays(inp):
    g = lambda n: np.asarray(inp[n])
    col = lambda n: g("L0_conv_" + n)[:REL].reshape(REL, 1)
    a = {}
    a["x"] = g("x").reshape(B, C, H * W)
    a["par32"] = np.concatenate([col(n) for n in ("b1", "b2", "bn1_g", "bn1_b", "bn1_m", "bn1_v", "bn2_g", "bn2_b", "bn2_m", "bn2_v", "cb2")]
                                + [g("L0_conv_b3").reshape(REL, SHARE)], axis=1)
    pc = lambda n: g("L0_conv_" + n)[REL:].reshape(2, 1)
    pp = np.concatenate([g("L0_conv_wp"), g("L0_conv_bp").reshape(2, 1), pc("bn1_g"), pc("bn1_b"), pc("bn1_m"), pc("bn1_v")], axis=1)
    a["parp"] = np.ascontiguousarray(np.broadcast_to(pp[:, None, :], (2, H, 7)))
    w3 = g("L0_conv_w3").reshape(REL, SHARE, C).transpose(1, 0, 2)
    w = np.concatenate([g("L0_conv_w1")[None], g("L0_conv_w2")[None], w3], axis=0)
    a["proj_w"] = np.ascontiguousarray(w.reshape(10, REL, 2, 128).transpose(3, 2, 0, 1))
    lin = np.linspace(-1.0, 1.0, W, dtype=np.float32)
    refl = np.pad(np.arange(W), PAD, mode="reflect")
    tap = np.stack([refl[j:j + W] for j in range(K7)])
    pw = np.stack([np.broadcast_to(lin, (K7, W)), lin[tap]]).reshape(1, 2, K7 * W)
    a["posw"] = np.ascontiguousarray(np.broadcast_to(pw, (2 * H, 2, K7 * W)))
    a["posh"] = np.concatenate([lin.reshape(H, 1), lin[tap].T], axis=1)
    a["cw1pT"] = np.ascontiguousarray(g("L0_conv_cw1")[:, REL:].T)
    for n, w in (("cw1_bd", g("L0_conv_cw1")[:, :REL].T), ("cw2_bd", g("L0_conv_cw2").T)):
        a[n] = np.zeros((B * REL, B * REL), np.float32)
        for b in range(B):
            a[n][b * REL:(b + 1) * REL, b * REL:(b + 1) * REL] = w
    a["group_avg"] = np.kron(np.eye(16, dtype=np.float32), np.full((8, 8), 0.125, np.float32))
    a["ident"] = np.eye(128, dtype=np.float32)
    return {k: np.ascontiguousarray(v) for k, v in a.items()}

def token_arrays(inp):
    g = lambda n: np.asarray(inp[n])
    a = {}
    qkv = g("L1_attn_qkv_w").reshape(3, HG, P, 2, P)
    a["wq"] = qkv[0].transpose(3, 2, 0, 1)
    k = qkv[1].reshape(HG, HPG, DH, 2, P)
    k = np.concatenate([k, k[:, :, :DH // 2]], axis=2).reshape(HG, -1, 2, P)
    a["wkv"] = np.concatenate([k, qkv[2]], axis=1).transpose(3, 2, 0, 1)
    bq = g("L1_attn_qkv_b").reshape(3, HG, P)
    k = bq[1].reshape(HG, HPG, DH)
    k = np.concatenate([k, k[:, :, :DH // 2]], axis=2).reshape(HG, -1)
    a["bk"] = np.broadcast_to(k[None], (P,) + k.shape)
    a["bv"] = bq[2].T
    a["bq"] = bq[0].T
    a["projw"] = g("L1_attn_proj_w").T.reshape(HG, P, C).transpose(1, 0, 2)
    a["projb"] = g("L1_attn_proj_b").reshape(2, P).T
    sel = np.zeros((3, DH, FT, 4, DH), np.float32)
    i = np.arange(DH)
    for r in range(DH // 2 + 1):
        sel[:, i, r // 4, r % 4, i] = 1
        sel[:, (i + r) % DH, r // 4, r % 4, i] = 1
    for r in (1, 2):
        sel[:, i, FT - 1, r, i] = 1
    a["sel"] = sel.reshape(3 * DH, FT, P)
    selb = np.zeros((P, 1), np.float32)
    selb[DH:2 * DH], selb[2 * DH:3 * DH], selb[3 * DH] = 1, -1, 1
    a["selb"] = selb
    a["heads"] = np.kron(np.eye(HPG, dtype=np.float32), np.ones((DH, DH), np.float32))
    a["avg"] = np.full((P, P), 1.0 / C, np.float32)
    a["wr"] = g("L1_ffn_wr").reshape(2, P).T
    a["br"] = np.broadcast_to(g("L1_ffn_br").reshape(1, 1), (P, 1))
    a["w1"] = g("L1_ffn_w1").reshape(2, P, 4 * C).transpose(1, 0, 2)
    a["b1"] = g("L1_ffn_b1").reshape(8, P).T
    a["w2"] = g("L1_ffn_w2").reshape(8, P, C).transpose(1, 0, 2)
    a["b2"] = g("L1_ffn_b2").reshape(2, P).T
    a["tri"] = np.triu(np.ones((P, P), np.float32), 1)
    return {k: np.ascontiguousarray(v) for k, v in a.items()}


def hybrid_kernel(nc, d, out):
    ctx = ExitStack()
    with ctx:
        planes = nc.dram_tensor("planes", (P, HP, SHARE, WP), F32, kind="Internal").ap()
        x2_dram = nc.dram_tensor("x2_dram", (P, HP, WP), F32, kind="Internal").ap()
        x1_dram = nc.dram_tensor("x1_dram", (P, S), F32, kind="Internal").ap()
        pf_dram = nc.dram_tensor("pf_dram", (6, K7, H, K7 * W), BF16, kind="Internal").ap()
        conv_dram = nc.dram_tensor("conv_dram", (B, C, S), F32, kind="Internal").ap()
        t2_dram = nc.dram_tensor("t2_dram", (B, C, S), F32, kind="Internal").ap()
        keep = {"ps": ctx.enter_context(nc.psum_tensor("ps", [P, 8, 512], F32)),
                "par": ctx.enter_context(nc.sbuf_tensor("par", [P, NPAR], F32)),
                "cw1p18": ctx.enter_context(nc.sbuf_tensor("cw1p18", [18, P], BF16))}
        for n in ("s1c", "t1c", "t2c", "s2c", "u2c"):
            keep[n] = ctx.enter_context(nc.sbuf_tensor(n, [P, 1], F32))
        project_stage(nc, d["x"], d["par32"], d["parp"], d["proj_w"], d["posw"], d["posh"], d["cw1pT"],
                      d["group_avg"], planes, x2_dram, x1_dram, pf_dram, keep)
        conv_stage(nc, planes, x2_dram, x1_dram, pf_dram, d["cw1_bd"], d["cw2_bd"], d["ident"], conv_dram, keep)
        attention_stage(nc, d["x"], conv_dram, t2_dram, d["wq"], d["wkv"], d["bk"], d["bv"], d["bq"], d["projw"], d["projb"],
                        d["sel"], d["selb"], d["heads"], d["avg"], d["ident"], keep)
        routed_stage(nc, t2_dram, out, d["wr"], d["br"], d["w1"], d["b1"], d["w2"], d["b2"], d["avg"], d["ident"],
                     d["tri"], keep)


def kernel(**inputs):
    import concourse.bacc as bacc
    from concourse.bass_utils import run_bass_kernel_spmd

    nc = bacc.Bacc("TRN2", target_bir_lowering=False, num_devices=1)
    arrays = {"in_" + k: v for k, v in (conv_arrays(inputs) | token_arrays(inputs)).items()}
    d = {k[3:]: nc.dram_tensor(k, v.shape, mybir.dt.from_np(v.dtype), kind="ExternalInput").ap() for k, v in arrays.items()}
    out = nc.dram_tensor("out_dram", (B, C, S), F32, kind="ExternalOutput").ap()
    hybrid_kernel(nc, d, out)
    r = run_bass_kernel_spmd(nc, [arrays], core_ids=[0])
    return r.results[0]["out_dram"].reshape(B, C, H, W)
```
